# Optimizing a Trainium2 kernel written in Bass

```python
import numpy as np
import jax
import jax.numpy as jnp

def _softmax(x, axis=-1):
    return jax.nn.softmax(x, axis=axis)

def _gelu(x):
    return jax.nn.gelu(x, approximate=True)

def _silu(x):
    return jax.nn.silu(x)

def _sigmoid(x):
    return jax.nn.sigmoid(x)

def _layernorm(x, axis=-1, eps=1e-05):
    m = jnp.mean(x, axis=axis, keepdims=True)
    v = jnp.var(x, axis=axis, keepdims=True)
    return (x - m) / jnp.sqrt(v + eps)

def _scatter_add(tgt, idx, src, axis=0):
    return tgt.at[idx].add(src)

def _segment_sum(src, seg, n):
    return jax.ops.segment_sum(src, seg, n)
kernel_name = 'mk_conv_preact_d1_conv_nhwc384_r2_fe2ccc'

def setup_inputs(seed: int=0):
    np.random.seed(seed)
    _w = jnp.asarray

    def _rec_inputs():
        import jax
        import jax.numpy as jnp
        _gk = jax.random.key(seed)
        x = -0.0001204 + 0.9999 * jax.random.normal(jax.random.fold_in(_gk, 1), (8, 56, 88, 192), jnp.float32)
        return x
    x = _rec_inputs()

    def _L0_conv_setup():
        import jax, jax.numpy as jnp
        import numpy as np
        WH, WW = (7, 11)
        NUM_HEADS = 8
        key = jax.random.key(seed)
        ks = jax.random.split(key, 5)
        B, H, W, C = (8, 56, 88, 192)
        x = jax.random.normal(ks[0], (B, H, W, C), dtype=jnp.float32)
        s = 1.0 / np.sqrt(C)
        qkv_w = jax.random.normal(ks[1], (C, 3 * C), dtype=jnp.float32) * s
        qkv_b = jax.random.normal(ks[2], (3 * C,), dtype=jnp.float32) * 0.02
        proj_w = jax.random.normal(ks[3], (C, C), dtype=jnp.float32) * s
        proj_b = jax.random.normal(ks[4], (C,), dtype=jnp.float32) * 0.02
        return {'x': x, 'qkv_w': qkv_w, 'qkv_b': qkv_b, 'proj_w': proj_w, 'proj_b': proj_b}
    _L0_conv_all = _L0_conv_setup()
    _L0_conv_in = {k: v for k, v in _L0_conv_all.items() if k in ('qkv_w', 'qkv_b', 'proj_w', 'proj_b')}
    del _L0_conv_all
    return {'x': x, 'L0_conv_qkv_w': _L0_conv_in['qkv_w'], 'L0_conv_qkv_b': _L0_conv_in['qkv_b'], 'L0_conv_proj_w': _L0_conv_in['proj_w'], 'L0_conv_proj_b': _L0_conv_in['proj_b']}

def reference(x, L0_conv_qkv_w, L0_conv_qkv_b, L0_conv_proj_w, L0_conv_proj_b):
    import jax
    import jax.numpy as jnp

    def _L0_conv_ref(x, qkv_w, qkv_b, proj_w, proj_b):
        import jax, jax.numpy as jnp
        import numpy as np
        WH, WW = (7, 11)
        NUM_HEADS = 8
        B, H, W, C = x.shape
        Wh, Ww = (WH, WW)
        nh = NUM_HEADS
        hd = C // nh
        pad_h = (Wh - H % Wh) % Wh
        pad_w = (Ww - W % Ww) % Ww
        xp = jnp.pad(x, ((0, 0), (0, pad_h), (0, pad_w), (0, 0)))
        Hp, Wp = (xp.shape[1], xp.shape[2])
        nH, nW = (Hp // Wh, Wp // Ww)
        xw = xp.reshape(B, nH, Wh, nW, Ww, C).transpose(0, 1, 3, 2, 4, 5)
        Bnw = B * nH * nW
        N = Wh * Ww
        xw = xw.reshape(Bnw, N, C)
        qkv = xw @ qkv_w + qkv_b
        q, k, v = jnp.split(qkv, 3, axis=-1)
        q = q.reshape(Bnw, N, nh, hd).transpose(0, 2, 1, 3)
        k = k.reshape(Bnw, N, nh, hd).transpose(0, 2, 1, 3)
        v = v.reshape(Bnw, N, nh, hd).transpose(0, 2, 1, 3)
        attn = jnp.einsum('bhnd,bhmd->bhnm', q, k) / jnp.sqrt(jnp.float32(hd)).astype(q.dtype)
        attn = jax.nn.softmax(attn, axis=-1)
        out = jnp.einsum('bhnm,bhmd->bhnd', attn, v)
        out = out.transpose(0, 2, 1, 3).reshape(Bnw, N, C)
        out = out @ proj_w + proj_b
        out = out.reshape(B, nH, nW, Wh, Ww, C).transpose(0, 1, 3, 2, 4, 5).reshape(B, Hp, Wp, C)
        if pad_h or pad_w:
            out = out[:, :H, :W, :]
        return out

    def _gn(v, G=32, eps=1e-05):
        B_, H_, W_, C_ = v.shape
        g = v.reshape(B_, H_, W_, G, C_ // G)
        m = jnp.mean(g, axis=(1, 2, 4), keepdims=True)
        s = jnp.var(g, axis=(1, 2, 4), keepdims=True)
        return ((g - m) / jnp.sqrt(s + eps)).reshape(v.shape)

    def _ln_c(v, eps=1e-06):
        m = jnp.mean(v, axis=-1, keepdims=True)
        s = jnp.var(v, axis=-1, keepdims=True)
        return (v - m) / jnp.sqrt(s + eps)

    def _ln_t(v, eps=1e-05):
        m = jnp.mean(v, axis=-1, keepdims=True)
        s = jnp.var(v, axis=-1, keepdims=True)
        return (v - m) / jnp.sqrt(s + eps)

    def _to_tokens(v):
        B_, H_, W_, C_ = v.shape
        return v.reshape(B_, H_ * W_, C_)

    def _from_tokens(t, like):
        return t.reshape(like.shape)
    x = x + _L0_conv_ref(_gn(x), L0_conv_qkv_w, L0_conv_qkv_b, L0_conv_proj_w, L0_conv_proj_b)
    return x

_drawn_inputs = setup_inputs


def setup_inputs(seed=0):
    import zlib

    import numpy as np

    out = dict(_drawn_inputs(seed))
    spreads = {}
    factors = {'L0_conv_qkv_b': 2.72, 'L0_conv_proj_b': 2.989}
    for name, (base, spread) in spreads.items():
        noise = np.random.default_rng([zlib.crc32(name.encode()), seed]).standard_normal(out[name].shape)
        drawn = base * np.exp(spread * noise) if base else spread * noise
        out[name] = jnp.asarray(drawn.astype(out[name].dtype))
    for name, factor in factors.items():
        out[name] = (out[name] * factor).astype(out[name].dtype)
    return out
```

```python
from contextlib import ExitStack

import concourse.bass as bass
from concourse import mybir

F32 = mybir.dt.float32
F32R = mybir.dt.float32r
ALU = mybir.AluOpType
ACT = mybir.ActivationFunctionType
AXIS = mybir.AxisListType

BATCH, HEIGHT, WIDTH, CH = 8, 56, 88, 192
WIN_H, WIN_W = 7, 11
TOK = WIN_H * WIN_W
TOKE = TOK + 1
HEADS, HD = 8, 24
GROUPS, GCH = 32, 6
EPS = 1e-5
NWC = WIDTH // WIN_W
STRIPS = 2
ROWS = STRIPS * WIN_H
PART = ROWS * NWC
BLOCKS = BATCH * HEIGHT // ROWS
BLOCKS_IMG = HEIGHT // ROWS
WINS = STRIPS * NWC
PAIRS = WINS // 2
N_PAIRS = BLOCKS * PAIRS
TILES = WIN_W
COLS = WINS * TOK
CA, CB = 128, CH - 128
ROW_G, NG, NJ = 32, 4, 2
AUG = HD + 1
STEP_TILES = [(0, 2), (2, 2), (4, 2), (6, 1), (7, 1), (8, 1), (9, 1), (10, 1)]
BODY = 2
SLOTS = BODY * PAIRS
LAST_IT = BLOCKS // BODY - 1
X_LEAD = PAIRS + 1
P_LAG = PAIRS + 1


def window_attention(nc, x, qkv_w, qkv_b, proj_w, proj_b, out):
    x_blk = x.rearrange("b (s r) (w c) d -> (b s) (r w) (c d)", r=ROWS, c=WIN_W)
    out_blk = out.rearrange("b (s r) (w c) d -> (b s) (r w) (c d)", r=ROWS, c=WIN_W)

    with ExitStack() as ctx:
        def sb(name, shape, dt=F32):
            return ctx.enter_context(nc.sbuf_tensor(name, shape, dt))

        def sem(name):
            return ctx.enter_context(nc.semaphore(name))

        ident = sb("ident", [128, 128])
        ident_r = sb("ident_r", [TOK, TOKE], F32R)
        ones = sb("ones", [128, PART])
        wA, wB = sb("wA", [CA, 3 * CH]), sb("wB", [128, 3 * CH])
        pA, pB = sb("pA", [CA, CH]), sb("pB", [128, CH])
        padA, padB = sb("padA", [CA, 4 * 128]), sb("padB", [128, 4 * 128])
        wqk = {k: sb(f"wqk_{k}", [128, 4 * 128], F32R) for k in ("hiA", "loA", "hiB", "loB")}
        wv = {k: sb(f"wv_{k}", [128, CH], F32R) for k in ("hiA", "loA", "hiB", "loB")}
        wp = {k: sb(f"wp_{k}", [128, CH], F32R) for k in ("hiA", "loA", "hiB", "loB")}
        b_qk = sb("b_qk", [128, 4])
        bvA, bvB, b_proj = sb("bvA", [CA, 1]), sb("bvB", [CB, 1]), sb("b_proj", [1, CH])
        bvA_rep, bvB_rep = sb("bvA_rep", [CA, PART]), sb("bvB_rep", [CB, PART])
        bias_out = sb("bias_out", [PART, CH])
        HALF = 2 * WIN_W
        x_stat = [sb(f"x_stat{h}", [PART, HALF, CH]) for h in range(2)]
        stat6 = sb("stat6", [PART, 2, GROUPS, 6])
        mean_all, var_all = sb("mean_all", [PART, BATCH * GROUPS]), sb("var_all", [PART, BATCH * GROUPS])
        rstd_all, newton = sb("rstd_all", [PART, BATCH * GROUPS]), sb("newton", [PART, BATCH * GROUPS])
        st_dev, st_sq = sb("st_dev", [PART, 2, GROUPS, 2]), sb("st_sq", [PART, 2, GROUPS, 2])
        st_sum = sb("st_sum", [PART, GROUPS])
        x_norm = [sb(f"x_norm{p}", [PART, TILES, CH]) for p in range(2)]
        y_blk = [sb(f"y_blk{p}", [PART, TILES, CH]) for p in range(2)]
        xT_hiA = [sb(f"xT_hiA{p}", [CA, COLS + 2], F32R) for p in range(2)]
        xT_loA = [sb(f"xT_loA{p}", [CA, COLS + 2], F32R) for p in range(2)]
        xT_B = [sb(f"xT_B{p}", [128, COLS + 2], F32R) for p in range(2)]
        oT_hiA = [sb(f"oT_hiA{p}", [CA, TILES, PART], F32R) for p in range(2)]
        oT_loA = [sb(f"oT_loA{p}", [CA, TILES, PART], F32R) for p in range(2)]
        oT_B = [sb(f"oT_B{p}", [128, TILES, PART], F32R) for p in range(2)]
        q_hi, q_lo = sb("q_hi", [128, 4, TOKE], F32R), sb("q_lo", [128, 4, TOKE], F32R)
        k_hi = [sb(f"k_hi{p}", [128, 4, TOKE], F32R) for p in range(2)]
        k_lo = [sb(f"k_lo{p}", [128, 4, TOKE], F32R) for p in range(2)]
        v_sb = [sb(f"v_sb{p}", [TOK, 2 * HEADS, HD + 1]) for p in range(2)]
        neg_max = sb("neg_max", [TOK, 4, NG, ROW_G], F32R)
        probs = sb("probs", [TOK, NG, 4, TOK])
        recip = sb("recip", [TOK, 2 * HEADS, 1])
        o_sb = sb("o_sb", [TOK, 2, CH])
        ps_s = ctx.enter_context(nc.psum_tensor("ps_s", [128, NG, 512], F32))
        ps_q = ctx.enter_context(nc.psum_tensor("ps_q", [128, 512], F32))
        ps_k = ctx.enter_context(nc.psum_tensor("ps_k", [128, 512], F32))
        ps_a = ctx.enter_context(nc.psum_tensor("ps_a", [128, 512], F32))
        ps_b = ctx.enter_context(nc.psum_tensor("ps_b", [128, 512], F32))

        pe_scores, pe_probs_in, pe_max = sem("pe_scores"), sem("pe_scoresT"), sem("pe_max_added")
        pe_q, pe_k, pe_v = sem("pe_q"), sem("pe_k"), sem("pe_v")
        pe_av, pe_oT, pe_proj, pe_xT = sem("pe_av"), sem("pe_oT"), sem("pe_proj"), sem("pe_xT")
        act_q, act_k, act_v, act_exp = sem("act_q"), sem("act_k"), sem("act_v"), sem("act_exp")
        act_oT, act_xT = sem("act_oT"), sem("act_xT")
        dve_max, dve_q, dve_k = sem("dve_max"), sem("dve_q"), sem("dve_k")
        dve_norm, dve_recip = sem("dve_norm"), sem("dve_recip")
        dve_oT, dve_xT, dve_out = sem("dve_oT"), sem("dve_xT"), sem("dve_out")
        pool_x, pool_y, pool_c = sem("pool_x"), sem("pool_y"), sem("pool_centred")
        dma_x = [sem(f"dma_x{p}") for p in range(2)]
        dma_y = [sem(f"dma_y{p}") for p in range(2)]
        dma_out = [sem(f"dma_out{p}") for p in range(2)]
        dma_w, dma_bqk, dma_stat = sem("dma_w"), sem("dma_bqk"), [sem("dma_stat0"), sem("dma_stat1")]
        pool_const, setup_w = sem("pool_const"), sem("setup_w")
        dve_stat, pe_stat, setup_chain = sem("dve_stat"), sem("pe_stat"), sem("setup_chain")
        stats_chain = sem("stats_chain")
        act_sqrt, stats_done, stat_read = sem("act_sqrt"), sem("stats_done"), sem("stat_read")
        pe_bias, setup_done = sem("pe_bias"), sem("setup_done")

        def reach(eng, semaphore, count):
            if isinstance(count, int) and count <= 0:
                return
            eng.wait_ge(semaphore, count)

        def exists(index, limit=N_PAIRS):
            return not isinstance(index, int) or 0 <= index < limit

        def parity(s):
            return (s // PAIRS) % 2

        def slots(eng, slot):
            for s in range(-X_LEAD, SLOTS):
                slot(0, s)
            with eng.Fori(1, LAST_IT) as it:
                base = eng.snap(it * SLOTS)
                for s in range(SLOTS):
                    slot(base, s)
            for s in range(SLOTS + P_LAG):
                slot(LAST_IT * SLOTS, s)

        def xT_tokens(t, r0, r1, c):
            return t[r0:r1, 0:COLS].rearrange("p (t w c r) -> p t w c r", t=STRIPS, w=NWC, c=WIN_W)[:, :, :, c, :]

        def xT_psum(c, chunk, r0, r1):
            at = (2 * c + chunk) * PART
            return ps_b[r0:r1, at:at + PART].rearrange("p (t r w) -> p t w r", t=STRIPS, r=WIN_H)

        def oT_tokens(t, r0, r1, w0):
            strip, w = (w0 // NWC) % STRIPS, w0 % NWC
            v = t[r0:r1, :, :].rearrange("p c (t r w) -> p t w c r", t=STRIPS, r=WIN_H)
            return v[:, strip, w:w + 2, :, :]

        def oT_psum(chunk, r0, r1):
            at = 2 * chunk * TOK
            return ps_b[r0:r1, at:at + 2 * TOK].rearrange("p (w c r) -> p w c r", w=2, c=WIN_W)

        block = ctx.enter_context(nc.Block())

        @block.sync
        def _(sp):
            sp.dma_start(wA[:, :], qkv_w[0:CA, :]).then_inc(dma_w, 16)
            sp.dma_start(wB[0:CB, :], qkv_w[CA:CH, :]).then_inc(dma_w, 16)
            sp.dma_start(wB[CB:128, :], qkv_w[CA:CH, :]).then_inc(dma_w, 16)
            sp.dma_start(pA[:, :], proj_w[0:CA, :]).then_inc(dma_w, 16)
            sp.dma_start(pB[0:CB, :], proj_w[CA:CH, :]).then_inc(dma_w, 16)
            sp.dma_start(pB[CB:128, :], proj_w[CA:CH, :]).then_inc(dma_w, 16)
            v_bias = qkv_b[2 * CH:3 * CH].rearrange("(c a) -> c a", a=1)
            sp.dma_start(bvA[:, :], v_bias[0:CA, :]).then_inc(dma_w, 16)
            sp.dma_start(bvB[:, :], v_bias[CA:CH, :]).then_inc(dma_w, 16)
            sp.dma_start(b_proj[:, :], proj_b.rearrange("(a c) -> a c", a=1)).then_inc(dma_w, 16)
            sp.wait_ge(pool_const, 4)
            qk_bias = qkv_b[0:2 * CH].rearrange("(sj g d) -> g d sj", g=NG, d=HD)
            for g in range(NG):
                sp.dma_start(b_qk[ROW_G * g:ROW_G * g + HD, :], qk_bias[g, :, :],
                             allow_slow_non_contiguous=True).then_inc(dma_bqk, 16)

            def load_half(b, h, reads):
                reach(sp, stat_read, reads)
                src = x_blk[bass.ds(b * BLOCKS_IMG + 2 * h, 2), :, :].rearrange("s p f -> p s f")
                sp.dma_start(x_stat[h][:, :, :].rearrange("p (s c) d -> p s (c d)", s=2), src)\
                    .then_inc(dma_stat[h], 16)

            for h in range(2):
                load_half(0, h, 0)
            with sp.Fori(1, BATCH) as b:
                reads = sp.snap(b * 2)
                for h in range(2):
                    load_half(b, h, reads + (h - 1))

            def load_x(c, par, count):
                reach(sp, pe_xT, count)
                sp.dma_start(x_norm[par][:, :, :].rearrange("p c d -> p (c d)"), x_blk[c, :, :])\
                    .then_inc(dma_x[par], 16)

            def store_y(c, par, rows_done):
                reach(sp, dve_out, rows_done)
                sp.dma_start(out_blk[c, :, :], y_blk[par][:, :, :].rearrange("p c d -> p (c d)"))\
                    .then_inc(dma_out[par], 16)

            def load_y(c, par, stored):
                reach(sp, dma_out[par], stored)
                sp.dma_start(y_blk[par][:, :, :].rearrange("p c d -> p (c d)"), x_blk[c, :, :])\
                    .then_inc(dma_y[par], 16)

            def step(base, blk, c):
                now = base + blk * PAIRS
                par = blk % 2
                if exists(now + 2 * PAIRS):
                    load_x(c + 2, par, now + PAIRS)
                if exists(now - 2 * PAIRS):
                    store_y(c - 2, par, now - PAIRS)
                if exists(now):
                    load_y(c, par, base + (blk // 2) * 16)

            for blk in range(-2, BODY):
                step(0, blk, blk)
            with sp.Fori(1, LAST_IT) as it:
                base = sp.snap(it * SLOTS)
                first = sp.snap(it * BODY)
                for blk in range(BODY):
                    step(base, blk, first + blk)
            for blk in range(BODY + 2):
                step(LAST_IT * SLOTS, blk, LAST_IT * BODY + blk)
            for p in range(2):
                sp.wait_ge(dma_out[p], 16 * (BLOCKS // 2))

        @block.gpsimd
        def _(pool):
            nc.gpsimd.memset(ident[:, :], 0.0).then_inc(pool_const, 1)
            nc.gpsimd.memset(b_qk[:, 0:2], 0.0).then_inc(pool_const, 1)
            nc.gpsimd.memset(b_qk[:, 2:4], 1.0).then_inc(pool_const, 1)
            nc.gpsimd.memset(ones[:, :], 1.0).then_inc(pool_const, 1)
            pool.wait_ge(pool_const, 4)
            nc.gpsimd.affine_select(out=ident[:, :], in_=ident[:, :], compare_op=ALU.not_equal, fill=1.0,
                                    base=0, pattern=[[-1, 128]], channel_multiplier=1).then_inc(pool_const, 1)
            pool.wait_ge(stats_done, 1)
            pool.wait_ge(setup_done, 1)

            def of_group(table, b):
                row = table[:, bass.ds(b * GROUPS, GROUPS)]
                return row.unsqueeze(1).unsqueeze(3).broadcast_to([PART, TILES, GROUPS, GCH])

            def normalise(b, par, loaded, base_count):
                x4 = x_norm[par][:, :, :].rearrange("p c (g k) -> p c g k", k=GCH)
                reach(pool, dma_x[par], loaded)
                nc.gpsimd.tensor_tensor(x4, x4, of_group(mean_all, b), ALU.subtract).then_inc(pool_c, PAIRS)
                reach(pool, pool_c, base_count)
                nc.gpsimd.tensor_tensor(x4, x4, of_group(rstd_all, b), ALU.mult).then_inc(pool_x, PAIRS)

            def add_bias(par, loaded):
                reach(pool, dma_y[par], loaded)
                y = y_blk[par][:, :, :]
                bias = bias_out[:, :].unsqueeze(1).broadcast_to([PART, TILES, CH])
                nc.gpsimd.tensor_tensor(y, y, bias, ALU.add).then_inc(pool_y, PAIRS)

            def step(base, blk, b_next):
                now = base + blk * PAIRS
                loads = base + (blk // 2) * 16
                if exists(now + 2 * PAIRS):
                    normalise(b_next, blk % 2, loads + 32, now + 3 * PAIRS)
                if exists(now):
                    add_bias(blk % 2, loads + 16)

            for blk in range(-2, BODY):
                step(0, blk, (blk + 2) // BLOCKS_IMG)
            with pool.Fori(1, LAST_IT) as it:
                base = pool.snap(it * SLOTS)
                b_next = pool.snap((it + 1) // 2)
                for blk in range(BODY):
                    step(base, blk, b_next)
            for blk in range(BODY):
                step(LAST_IT * SLOTS, blk, BATCH - 1)

        @block.scalar
        def _(act):
            act.wait_ge(dve_stat, 2 * BATCH + 1)
            nc.scalar.activation(rstd_all[:, :], var_all[:, :], ACT.Sqrt).then_inc(act_sqrt, 1)
            act.wait_ge(setup_done, 1)

            def slot(base, s):
                i = base + s
                k_now, now = (s + 1) % 2, parity(s - 1)
                if exists(i + 1):
                    reach(act, pe_k, i + 2)
                    for j in range(NJ):
                        last = nc.scalar.activation(k_hi[k_now][:, 2 * j:2 * j + 2, :],
                                                    ps_k[:, 0:4 * TOKE].rearrange("p (a n) -> p a n", a=4)[:, 2 * j:2 * j + 2, :],
                                                    ACT.Identity, bias=b_qk[:, 2 + j:3 + j])
                    last.then_inc(act_k, 1)
                if exists(i):
                    reach(act, pe_probs_in, i + 1)
                    nc.scalar.activation(probs[:, :, :, :],
                                         ps_s[0:TOK, :, 0:4 * TOKE].rearrange("p g (a n) -> p g a n", a=4)[:, :, :, 0:TOK],
                                         ACT.Exp, scale=float(HD) ** -0.5).then_inc(act_exp, 1)
                if exists(i - 1):
                    reach(act, pe_oT, i)
                    w0 = 2 * (s - 1)
                    for chunk, r0, dst in ((0, 0, oT_hiA[now]), (1, CB, oT_B[now])):
                        last = nc.scalar.activation(oT_tokens(dst, r0, 128, w0), oT_psum(chunk, r0, 128), ACT.Copy)
                    last.then_inc(act_oT, 1)
                if exists(i + 1):
                    reach(act, pe_q, i + 2)
                    for j in range(NJ):
                        last = nc.scalar.activation(q_hi[:, 2 * j:2 * j + 2, :],
                                                    ps_q[:, 0:4 * TOKE].rearrange("p (a n) -> p a n", a=4)[:, 2 * j:2 * j + 2, :],
                                                    ACT.Identity, bias=b_qk[:, j:j + 1])
                    last.then_inc(act_q, 1)
                    reach(act, pe_v, i + 2)
                    nc.scalar.activation(v_sb[k_now][:, :, 0:HD],
                                         ps_a[0:TOK, 0:2 * CH].rearrange("p (h d) -> p h d", d=HD),
                                         ACT.Copy).then_inc(act_v, 1)
                if exists(i + X_LEAD):
                    reach(act, pe_xT, i + X_LEAD + 1)
                    t0, n = STEP_TILES[(s + X_LEAD) % PAIRS]
                    buf = parity(s + X_LEAD)
                    for c in range(n):
                        for chunk, r0, dst in ((0, 0, xT_hiA[buf]), (1, CB, xT_B[buf])):
                            last = nc.scalar.activation(xT_tokens(dst, r0, 128, t0 + c), xT_psum(c, chunk, r0, 128),
                                                        ACT.Copy)
                    last.then_inc(act_xT, 1)

            slots(act, slot)

        @block.vector
        def _(dve):
            chained = [0]

            def link(instruction):
                chained[0] += 1
                instruction.then_inc(setup_chain, 1)
                dve.wait_ge(setup_chain, chained[0])

            tt, ts = nc.vector.tensor_tensor, nc.vector.tensor_scalar
            nc.vector.memset(padA[:, :], 0.0)
            nc.vector.memset(padB[:, :], 0.0)
            nc.vector.memset(neg_max[:, :, :, :].bitcast(mybir.dt.uint32), 0)
            for p in range(2):
                nc.vector.memset(v_sb[p][:, :, HD:HD + 1], 1.0)
                for t in (xT_hiA, xT_loA, xT_B):
                    last = nc.vector.memset(t[p][:, COLS:COLS + 2].bitcast(mybir.dt.uint32), 0)
            link(last)
            dve.wait_ge(dma_w, 9 * 16)
            for w, pad in ((wA, padA), (wB, padB)):
                last = nc.vector.tensor_copy(
                    pad[:, :].rearrange("p (h e) -> p h e", e=ROW_G)[:, :, 0:HD],
                    w[:, 0:2 * CH].rearrange("p (h d) -> p h d", d=HD))
            link(last)
            for srcA, srcB, dst in ((padA[:, :], padB[:, :], wqk), (wA[:, 2 * CH:], wB[:, 2 * CH:], wv),
                                    (pA[:, :], pB[:, :], wp)):
                for src, hi, lo in ((srcA, dst["hiA"], dst["loA"]), (srcB, dst["hiB"], dst["loB"])):
                    link(nc.vector.tensor_copy(hi[:, :], src))
                    last = tt(lo[:, :], src, hi[:, :].bitcast(F32), ALU.subtract)
            nc.vector.tensor_copy(bvA_rep[:, :], bvA[:, 0:1].broadcast_to([CA, PART]))
            nc.vector.tensor_copy(bvB_rep[:, :], bvB[:, 0:1].broadcast_to([CB, PART]))
            dve.wait_ge(pool_const, 5)
            nc.vector.tensor_copy(ident_r[:, :], ident[0:TOK, 0:TOKE]).then_inc(setup_w, 1)
            dve.wait_ge(pe_bias, 1)
            nc.vector.tensor_copy(bias_out[:, :], ps_a[0:PART, 0:CH]).then_inc(setup_w, 1)

            n_part = HALF * GCH // 2
            mean_v = stat6[:, :, :, :].rearrange("p h g (e t) -> p h g e t", e=2)[:, :, :, :, 1]
            m2_v = stat6[:, :, :, :].rearrange("p h g (e t) -> p h g e t", e=2)[:, :, :, :, 2]
            STEPS = 6

            def stats_of(b):
                done = [0]

                def step(instruction):
                    done[0] += 1
                    instruction.then_inc(stats_chain, 1)
                    dve.wait_ge(stats_chain, b * STEPS + done[0])

                for h in range(2):
                    dve.wait_ge(dma_stat[h], b * 16 + 16)
                    for g in range(GROUPS):
                        last = nc.vector.bn_stats(stat6[:, h, g, :], x_stat[h][:, :, GCH * g:GCH * (g + 1)])
                    last.then_inc(stat_read, 1)
                dve.wait_ge(pe_stat, b * 2 + 1)
                step(nc.vector.tensor_reduce(st_sum[:, :], stat_sum_view(), AXIS.XY, ALU.add))
                mean_b = mean_all[:, bass.ds(b * GROUPS, GROUPS)]
                step(ts(mean_b, st_sum[:, :], 1.0 / (4 * PART), None, ALU.mult))
                step(tt(st_dev[:, :, :, :], mean_v,
                        mean_b.unsqueeze(1).unsqueeze(3).broadcast_to([PART, 2, GROUPS, 2]), ALU.subtract))
                step(tt(st_sq[:, :, :, :], st_dev[:, :, :, :], st_dev[:, :, :, :], ALU.mult))
                nc.vector.scalar_tensor_tensor(out=st_dev[:, :, :, :], in0=st_sq[:, :, :, :], scalar=float(n_part),
                                               in1=m2_v, op0=ALU.mult, op1=ALU.add).then_inc(dve_stat, 2)
                dve.wait_ge(pe_stat, b * 2 + 2)
                step(nc.vector.tensor_reduce(st_sum[:, :], stat_sum_view(), AXIS.XY, ALU.add))
                step(ts(var_all[:, bass.ds(b * GROUPS, GROUPS)], st_sum[:, :], 1.0 / (4 * PART * n_part), EPS,
                        ALU.mult, ALU.add))

            def stat_sum_view():
                return ps_b[0:PART, 0:4 * GROUPS].rearrange("p (h g e) -> p g h e", h=2, g=GROUPS)

            with dve.Fori(0, BATCH) as b:
                stats_of(b)
            nc.vector.nop().then_inc(dve_stat, 1)
            dve.wait_ge(act_sqrt, 1)
            link(nc.vector.reciprocal(rstd_all[:, :], rstd_all[:, :]))
            link(tt(newton[:, :], rstd_all[:, :], rstd_all[:, :], ALU.mult))
            link(tt(newton[:, :], newton[:, :], var_all[:, :], ALU.mult))
            link(ts(newton[:, :], newton[:, :], -0.5, 1.5, ALU.mult, ALU.add))
            tt(rstd_all[:, :], rstd_all[:, :], newton[:, :], ALU.mult).then_inc(stats_done, 1)
            dve.wait_ge(dma_bqk, NG * 16)
            nc.vector.nop().then_inc(setup_done, 1)

            def lo_part(dst, psum, hi, bias=None):
                if bias is None:
                    return tt(dst, psum, hi.bitcast(F32), ALU.subtract)
                return nc.vector.scalar_tensor_tensor(out=dst, in0=psum, scalar=bias, in1=hi.bitcast(F32),
                                                      op0=ALU.add, op1=ALU.subtract)

            def slot(base, s):
                i = base + s
                now = parity(s - 1)
                if exists(i):
                    reach(dve, pe_scores, i + 1)
                    nc.vector.tensor_reduce(
                        neg_max[:, :, :, HD:HD + 1].rearrange("p a g e -> p g (a e)"),
                        ps_s[0:TOK, :, 0:4 * TOKE].rearrange("p g (a n) -> p g a n", a=4)[:, :, :, 0:TOK],
                        AXIS.X, ALU.max, negate=True).then_inc(dve_max, 1)
                    reach(dve, pe_max, i + 1)
                    for j in range(NJ):
                        last = lo_part(q_lo[:, 2 * j:2 * j + 2, :],
                                       ps_q[:, 0:4 * TOKE].rearrange("p (a n) -> p a n", a=4)[:, 2 * j:2 * j + 2, :],
                                       q_hi[:, 2 * j:2 * j + 2, :], b_qk[:, j:j + 1])
                    last.then_inc(dve_q, 1)
                if exists(i - 1):
                    reach(dve, pe_av, i)
                    av = ps_a[0:TOK, 0:2 * HEADS * (HD + 1)].rearrange("p (h e) -> p h e", e=HD + 1)
                    nc.vector.reciprocal(recip[:, :, :], av[:, :, HD:HD + 1]).then_inc(dve_recip, 1)
                    reach(dve, dve_recip, i)
                    tt(o_sb[:, :, :].rearrange("p w (h d) -> p (w h) d", d=HD), av[:, :, 0:HD],
                       recip[:, :, :].broadcast_to([TOK, 2 * HEADS, HD]), ALU.mult).then_inc(dve_norm, 1)
                if exists(i + 1):
                    reach(dve, act_k, i + 2)
                    k_now = (s + 1) % 2
                    for j in range(NJ):
                        last = lo_part(k_lo[k_now][:, 2 * j:2 * j + 2, :],
                                       ps_k[:, 0:4 * TOKE].rearrange("p (a n) -> p a n", a=4)[:, 2 * j:2 * j + 2, :],
                                       k_hi[k_now][:, 2 * j:2 * j + 2, :], b_qk[:, 2 + j:3 + j])
                    last.then_inc(dve_k, 1)
                if exists(i - P_LAG):
                    step, buf = (s - P_LAG) % PAIRS, parity(s - P_LAG)
                    t0, n = STEP_TILES[step]
                    reach(dve, pe_proj, i - P_LAG + 1)
                    if step == 0:
                        reach(dve, pool_y, i - P_LAG + PAIRS)
                    y = y_blk[buf][:, t0:t0 + n, :]
                    tt(y, ps_b[0:PART, 0:n * CH].rearrange("p (c d) -> p c d", d=CH), y, ALU.add)\
                        .then_inc(dve_out, 1)
                if exists(i - 1):
                    reach(dve, act_oT, i)
                    w0 = 2 * (s - 1)
                    lo_part(oT_tokens(oT_loA[now], 0, 128, w0), oT_psum(0, 0, 128), oT_tokens(oT_hiA[now], 0, 128, w0))
                    lo_part(oT_tokens(oT_B[now], 0, CB, w0), oT_psum(1, CB, 128),
                            oT_tokens(oT_B[now], CB, 128, w0)).then_inc(dve_oT, 1)
                if exists(i + X_LEAD):
                    reach(dve, act_xT, i + X_LEAD + 1)
                    t0, n = STEP_TILES[(s + X_LEAD) % PAIRS]
                    buf = parity(s + X_LEAD)
                    for c in range(n):
                        lo_part(xT_tokens(xT_loA[buf], 0, 128, t0 + c), xT_psum(c, 0, 0, 128),
                                xT_tokens(xT_hiA[buf], 0, 128, t0 + c))
                        last = lo_part(xT_tokens(xT_B[buf], 0, CB, t0 + c), xT_psum(c, 1, CB, 128),
                                       xT_tokens(xT_B[buf], CB, 128, t0 + c))
                    last.then_inc(dve_xT, 1)

            slots(dve, slot)

        @block.tensor
        def _(pe):
            mm = nc.tensor.matmul
            pe.wait_ge(setup_w, 1)
            mm(ps_a[0:PART, 0:CH], bvA_rep[:, :], pA[:, :], start=True, stop=False)
            mm(ps_a[0:PART, 0:CH], bvB_rep[:, :], pB[0:CB, :], start=False, stop=False)
            mm(ps_a[0:PART, 0:CH], ones[0:1, :], b_proj[:, :], start=False, stop=True).then_inc(pe_bias, 1)

            mean_v = stat6[:, :, :, :].rearrange("p h g (e t) -> p (h g) e t", e=2)[:, :, :, 1]
            with pe.Fori(0, BATCH) as b:
                pe.wait_ge(stat_read, b * 2 + 2)
                mm(ps_b[0:PART, 0:4 * GROUPS].rearrange("p (a e) -> p a e", e=2), ones[0:PART, :], mean_v,
                   start=True, stop=True).then_inc(pe_stat, 1)
                pe.wait_ge(dve_stat, b * 2 + 2)
                mm(ps_b[0:PART, 0:4 * GROUPS], ones[0:PART, :],
                   st_dev[:, :, :, :].rearrange("p h g e -> p (h g e)"), start=True, stop=True).then_inc(pe_stat, 1)
            pe.wait_ge(setup_w, 2)
            pe.wait_ge(setup_done, 1)

            def products(dst, pairs, first=True, closes=True):
                for n, (lhsT, rhs) in enumerate(pairs):
                    last = mm(dst, lhsT, rhs, start=first and n == 0, stop=closes and n == len(pairs) - 1,
                              skip_group_check=True)
                return last

            def qk_chunks(bank, which, s, semaphore):
                buf, pair = parity(s), s % PAIRS
                for j in range(NJ):
                    col = 128 * (2 * which + j)

                    def w(part, row0=0):
                        return wqk[part][row0:128, col:col + 128]

                    for win in range(2):
                        at = (2 * pair + win) * TOK
                        last = products(ps_slice(bank, 2 * j + win), (
                            (w("hiA"), xT_hiA[buf][:, at:at + TOKE]), (w("loA"), xT_hiA[buf][:, at:at + TOKE]),
                            (w("hiA"), xT_loA[buf][:, at:at + TOKE]), (w("hiB"), xT_B[buf][:, at:at + TOKE]),
                            (w("loB", CB), xT_B[buf][CB:128, at:at + TOKE])), first=j == 0 and win == 0)
                last.then_inc(semaphore, 1)

            def ps_slice(bank, a):
                return bank[:, a * TOKE:(a + 1) * TOKE]

            def rows(g, n=AUG):
                return slice(ROW_G * g, ROW_G * g + n)

            def slot(base, s):
                i = base + s
                kb, kb_next, kb_prev = s % 2, (s + 1) % 2, (s - 1) % 2
                if exists(i):
                    reach(pe, act_q, i + 1)
                    reach(pe, act_k, i + 1)
                    reach(pe, act_exp, i)
                    for w in range(2):
                        for j in range(NJ):
                            for g in range(NG):
                                at = (2 * w + j) * TOKE
                                last = mm(ps_s[0:TOK, g, at:at + TOKE], q_hi[rows(g), 2 * j + w, 0:TOK],
                                          k_hi[kb][rows(g), 2 * j + w, :], start=True, stop=True)
                    last.then_inc(pe_scores, 1)
                if exists(i - 1):
                    reach(pe, act_exp, i)
                    reach(pe, act_v, (i + 1) if exists(i) else i)
                    for w in range(2):
                        for j in range(NJ):
                            for g in range(NG):
                                h = HEADS * w + NG * j + g
                                last = mm(ps_a[0:TOK, h * (HD + 1):(h + 1) * (HD + 1)], probs[:, g, 2 * w + j, :],
                                          v_sb[kb_prev][:, h, :], start=True, stop=True)
                    last.then_inc(pe_av, 1)
                if exists(i):
                    reach(pe, dve_max, i + 1)
                    for w in range(2):
                        for j in range(NJ):
                            last = mm(ps_slice(ps_q, 2 * j + w),
                                      neg_max[:, 2 * w + j, :, :].rearrange("p g e -> p (g e)"), ident_r[:, :],
                                      start=False, stop=True, skip_group_check=True)
                    last.then_inc(pe_max, 1)
                if exists(i + 1):
                    reach(pe, dve_k, i + 1)
                    if (s + 1) % PAIRS == 0:
                        reach(pe, act_xT, i + 1 + PAIRS)
                        reach(pe, dve_xT, i + 1 + PAIRS)
                    qk_chunks(ps_k, 1, s + 1, pe_k)
                if exists(i - P_LAG):
                    reach(pe, act_xT, min(i + X_LEAD, N_PAIRS) if isinstance(i, int) else i + X_LEAD)
                    reach(pe, dve_xT, min(i + X_LEAD, N_PAIRS) if isinstance(i, int) else i + X_LEAD)
                    step, buf = (s - P_LAG) % PAIRS, parity(s - P_LAG)
                    reach(pe, act_oT, min(i - 1, N_PAIRS) if isinstance(i, int) else i - 1)
                    reach(pe, dve_oT, min(i - 1, N_PAIRS) if isinstance(i, int) else i - 1)
                    if not exists(i - 2):
                        reach(pe, dve_out, i - P_LAG)
                    t0, n = STEP_TILES[step]
                    for c in range(n):
                        t = t0 + c
                        last = products(ps_b[0:PART, c * CH:(c + 1) * CH], (
                            (oT_hiA[buf][:, t, :], wp["hiA"][:, :]), (oT_hiA[buf][:, t, :], wp["loA"][:, :]),
                            (oT_loA[buf][:, t, :], wp["hiA"][:, :]), (oT_B[buf][:, t, :], wp["hiB"][:, :]),
                            (oT_B[buf][CB:128, t, :], wp["loB"][CB:128, :])))
                    last.then_inc(pe_proj, 1)
                if exists(i):
                    reach(pe, dve_q, i + 1)
                    for w in range(2):
                        for j in range(NJ):
                            a = 2 * j + w
                            for n, (k, q) in enumerate(((k_hi[kb], q_hi), (k_lo[kb], q_hi), (k_hi[kb], q_lo))):
                                for g in range(NG):
                                    at = (2 * w + j) * TOKE
                                    last = mm(ps_s[0:TOK, g, at:at + TOKE], k[rows(g), a, 0:TOK], q[rows(g), a, :],
                                              start=n == 0, stop=n == 2)
                    last.then_inc(pe_probs_in, 1)
                if exists(i - 1):
                    reach(pe, dve_norm, i)
                    reach(pe, dve_out, i - P_LAG + 1)
                    for w in range(2):
                        nc.tensor.transpose(ps_b[:, w * TOK:(w + 1) * TOK], o_sb[:, w, 0:CA], ident[0:TOK, 0:TOK])
                    for w in range(2):
                        last = nc.tensor.transpose(ps_b[:, (2 + w) * TOK:(3 + w) * TOK], o_sb[:, w, CB:CH],
                                                   ident[0:TOK, 0:TOK])
                    last.then_inc(pe_oT, 1)
                if exists(i + 1):
                    reach(pe, dve_q, i + 1)
                    qk_chunks(ps_q, 0, s + 1, pe_q)
                    reach(pe, dve_norm, i)
                    buf, pair = parity(s + 1), (s + 1) % PAIRS
                    for w in range(2):
                        at = (2 * pair + w) * TOK
                        hiA, loA, xB = (t[buf][:, at:at + TOK] for t in (xT_hiA, xT_loA, xT_B))
                        last = products(ps_a[0:TOK, w * CH:(w + 1) * CH], (
                            (hiA, wv["hiA"][:, :]), (hiA, wv["loA"][:, :]), (loA, wv["hiA"][:, :]),
                            (xB, wv["hiB"][:, :]), (xB[CB:128, :], wv["loB"][CB:128, :])))
                    last.then_inc(pe_v, 1)
                if exists(i + X_LEAD):
                    reach(pe, act_oT, i)
                    reach(pe, dve_oT, i)
                    reach(pe, dve_xT, i + X_LEAD)
                    step, buf = (s + X_LEAD) % PAIRS, parity(s + X_LEAD)
                    if step == 0:
                        reach(pe, pool_x, i + X_LEAD + PAIRS)
                    t0, n = STEP_TILES[step]
                    for c in range(n):
                        xt = x_norm[buf][:, t0 + c, :]
                        nc.tensor.transpose(ps_b[:, 2 * c * PART:(2 * c + 1) * PART], xt[:, 0:CA],
                                            ident[0:PART, 0:PART])
                        last = nc.tensor.transpose(ps_b[:, (2 * c + 1) * PART:(2 * c + 2) * PART], xt[:, CB:CH],
                                                   ident[0:PART, 0:PART])
                    last.then_inc(pe_xT, 1)

            slots(pe, slot)


def kernel(x, L0_conv_qkv_w, L0_conv_qkv_b, L0_conv_proj_w, L0_conv_proj_b):
    import numpy as np
    import concourse.bacc as bacc
    from concourse.bass_utils import run_bass_kernel_spmd

    nc = bacc.Bacc("TRN2", target_bir_lowering=False, num_devices=1)
    given = {"x": x, "qkv_w": L0_conv_qkv_w, "qkv_b": L0_conv_qkv_b, "proj_w": L0_conv_proj_w, "proj_b": L0_conv_proj_b}
    arrays = {f"in_{name}": np.ascontiguousarray(a) for name, a in given.items()}
    args = [nc.dram_tensor(name, a.shape, mybir.dt.from_np(a.dtype), kind="ExternalInput").ap()
            for name, a in arrays.items()]
    out = nc.dram_tensor("out", (BATCH, HEIGHT, WIDTH, CH), F32, kind="ExternalOutput").ap()
    window_attention(nc, *args, out)
    result = run_bass_kernel_spmd(nc, [arrays], core_ids=[0])
    return result.results[0]["out"]
```

```python
import math
from contextlib import ExitStack

import concourse.bass as bass
from concourse import mybir

F32 = mybir.dt.float32
F32R = mybir.dt.float32r
F16 = mybir.dt.float16
ALU = mybir.AluOpType
ACT = mybir.ActivationFunctionType
AXIS = mybir.AxisListType
RMAX = bass.bass_isa.ReduceOp.max

BATCH, HEIGHT, WIDTH, CH = 8, 56, 88, 192
WIN_H, WIN_W = 7, 11
TOK = WIN_H * WIN_W
TOKE = TOK + 1
HEADS, HD = 8, 24
GROUPS, GCH = 32, 6
EPS = 1e-5
NWC = WIDTH // WIN_W
STRIPS = 2
ROWS = STRIPS * WIN_H
PART = ROWS * NWC
BLOCKS = BATCH * HEIGHT // ROWS
BLOCKS_IMG = HEIGHT // ROWS
WINS = STRIPS * NWC
PAIRS = WINS // 2
N_PAIRS = BLOCKS * PAIRS
TILES = WIN_W
COLS = WINS * TOK
CA, CB = 128, CH - 128
ROW_G, NG, NJ = 32, 4, 2
AUG = HD + 1
STEP_TILES = [(0, 2), (2, 2), (4, 2), (6, 1), (7, 1), (8, 1), (9, 1), (10, 1)]
BODY = 2
SLOTS = BODY * PAIRS
LAST_IT = BLOCKS // BODY - 1
PREP_LEAD = PAIRS + 2
X_LEAD = PAIRS + 1
O_LAG = 2
P_LAG = PAIRS + O_LAG
Y_LAG = PAIRS - 2
V_BUFS = 4
FULL = 128
PAD = FULL - TOK
AUG_ONE = 32768.0
MARGIN = 4.0
LOG_SHIFT = math.log(64.0)
A_HI, B_BOTH, A_LO = range(3)


def window_attention(nc, x, qkv_w, qkv_b, proj_w, proj_b, out):
    x_blk = x.rearrange("b (s r) (w c) d -> (b s) (r w) (c d)", r=ROWS, c=WIN_W)
    out_blk = out.rearrange("b (s r) (w c) d -> (b s) (r w) (c d)", r=ROWS, c=WIN_W)

    with ExitStack() as ctx:
        def sb(name, shape, dt=F32):
            return ctx.enter_context(nc.sbuf_tensor(name, shape, dt))

        def sem(name):
            return ctx.enter_context(nc.semaphore(name))

        ident = sb("ident", [128, 128])
        ident16 = sb("ident16", [128, 128], F16)
        ident_aug = sb("ident_aug", [TOK, TOKE], F32R)
        ones = sb("ones", [128, PART])
        wA, wB = sb("wA", [CA, 3 * CH]), sb("wB", [128, 3 * CH])
        pA, pB = sb("pA", [CA, CH]), sb("pB", [128, CH])
        PARTS = ("hiA", "loA", "hiB", "loB")
        wqk = {k: sb(f"wqk_{k}", [128, 4, NG, ROW_G], F16) for k in PARTS}
        wv = {k: sb(f"wv_{k}", [128, CH], F16) for k in PARTS}
        wp = {k: sb(f"wp_{k}", [128, CH], F16) for k in PARTS}
        b_qk, aug, zeros = sb("b_qk", [128, 4]), sb("aug", [128, 4]), sb("zeros", [128, 4])
        bvA, bvB, b_proj = sb("bvA", [CA, 1]), sb("bvB", [CB, 1]), sb("b_proj", [1, CH])
        bvA_rep, bvB_rep = sb("bvA_rep", [CA, PART]), sb("bvB_rep", [CB, PART])
        bias_out = sb("bias_out", [PART, CH])
        big_parts, big_own, big = sb("big_parts", [128, 4, 3]), sb("big_own", [128, 4]), sb("big", [128, 4])
        big_inv = sb("big_inv", [128, 4])
        exp_scale, out_scale, exp_shift = sb("exp_scale", [128, 1]), sb("out_scale", [128, 1]), sb("exp_shift", [128, 1])
        HALF = 2 * WIN_W
        x_stat = [sb(f"x_stat{h}", [PART, HALF, CH]) for h in range(2)]
        stat6 = sb("stat6", [PART, 2, GROUPS, 6])
        mean_all, var_all = sb("mean_all", [PART, BATCH * GROUPS]), sb("var_all", [PART, BATCH * GROUPS])
        rstd_all, newton = sb("rstd_all", [PART, BATCH * GROUPS]), sb("newton", [PART, BATCH * GROUPS])
        st_dev, st_sq = sb("st_dev", [PART, 2, GROUPS, 2]), sb("st_sq", [PART, 2, GROUPS, 2])
        st_sum = sb("st_sum", [PART, GROUPS])
        x_norm = [sb(f"x_norm{p}", [PART, TILES, CH]) for p in range(2)]
        x_split = [sb(f"x_split{p}", [PART, TILES, 2 * CH], F16) for p in range(2)]
        y_blk = [sb(f"y_blk{p}", [PART, TILES, CH]) for p in range(2)]
        xT = [sb(f"xT{p}", [128, 3, COLS + PAD], F16) for p in range(2)]
        oT = [sb(f"oT{p}", [128, 3, TILES, PART], F16) for p in range(2)]
        def sb_qk(name):
            return sb(name, [128, 4 * TOKE + PAD], F16)

        q_hi, q_lo = sb_qk("q_hi"), sb_qk("q_lo")
        k_hi = [sb_qk(f"k_hi{p}") for p in range(2)]
        k_lo = [sb_qk(f"k_lo{p}") for p in range(2)]
        v_hi = [sb(f"v_hi{p}", [TOK, 2 * HEADS, HD + 1], F16) for p in range(V_BUFS)]
        v_lo = [sb(f"v_lo{p}", [TOK, 2 * HEADS, HD + 1], F16) for p in range(V_BUFS)]
        neg_max = sb("neg_max", [TOK, 4, NG, ROW_G], F32R)
        probs = sb("probs", [TOK, NG * 4 * TOK])
        p_hi = [sb(f"p_hi{p}", [TOK, NG * 4 * TOK + PAD], F16) for p in range(2)]
        p_lo = sb("p_lo", [TOK, NG * 4 * TOK + PAD], F16)
        recip = sb("recip", [TOK, 2 * HEADS, 1])
        o_sb = sb("o_sb", [TOK, 2, CH])
        o_split = sb("o_split", [TOK, 2, 2 * CH], F16)
        ps_s = ctx.enter_context(nc.psum_tensor("ps_s", [128, NG, 512], F32))
        ps_q = ctx.enter_context(nc.psum_tensor("ps_q", [128, 512], F32))
        ps_k = ctx.enter_context(nc.psum_tensor("ps_k", [128, 512], F32))
        ps_a = ctx.enter_context(nc.psum_tensor("ps_a", [128, 512], F32))
        ps_b = ctx.enter_context(nc.psum_tensor("ps_b", [128, 512], F32))
        ps_b16 = ps_b[:, :].bitcast(F16)

        pe_scores, pe_scoresT, pe_max = sem("pe_scores"), sem("pe_scoresT"), sem("pe_max_added")
        pe_q, pe_k, pe_v = sem("pe_q"), sem("pe_k"), sem("pe_v")
        pe_av, pe_oT, pe_proj, pe_xT = sem("pe_av"), sem("pe_oT"), sem("pe_proj"), sem("pe_xT")
        act_q, act_k, act_v, act_exp = sem("act_q"), sem("act_k"), sem("act_v"), sem("act_exp")
        act_o, act_xT = sem("act_o"), sem("act_xT")
        dve_max, dve_q, dve_k, dve_v = sem("dve_max"), sem("dve_q"), sem("dve_k"), sem("dve_v")
        dve_norm, dve_recip = sem("dve_norm"), sem("dve_recip")
        dve_oT, dve_out = sem("dve_oT"), sem("dve_out")
        pool_p, pool_o, pool_x, pool_y = sem("pool_p"), sem("pool_o"), sem("pool_x"), sem("pool_y")
        dma_x = [sem(f"dma_x{p}") for p in range(2)]
        dma_y = [sem(f"dma_y{p}") for p in range(2)]
        dma_out = [sem(f"dma_out{p}") for p in range(2)]
        pool_x_steps, pool_passed = sem("pool_x_steps"), sem("pool_passed")
        dma_w, dma_bqk, dma_stat = sem("dma_w"), sem("dma_bqk"), [sem("dma_stat0"), sem("dma_stat1")]
        pool_const, setup_w = sem("pool_const"), sem("setup_w")
        weights_big = sem("weights_big")
        dve_stat, pe_stat, setup_chain = sem("dve_stat"), sem("pe_stat"), sem("setup_chain")
        stats_chain = sem("stats_chain")
        act_sqrt, stats_done, stat_read = sem("act_sqrt"), sem("stats_done"), sem("stat_read")
        pe_bias, setup_done = sem("pe_bias"), sem("setup_done")

        def reach(eng, semaphore, count):
            if isinstance(count, int) and count <= 0:
                return
            eng.wait_ge(semaphore, count)

        def exists(index, limit=N_PAIRS):
            return not isinstance(index, int) or 0 <= index < limit

        def parity(s):
            return (s // PAIRS) % 2

        def slots(eng, slot):
            for s in range(-PREP_LEAD, SLOTS):
                slot(0, s)
            with eng.Fori(1, LAST_IT) as it:
                base = eng.snap(it * SLOTS)
                for s in range(SLOTS):
                    slot(base, s)
            for s in range(SLOTS + P_LAG + 1):
                slot(LAST_IT * SLOTS, s)

        def xT_tokens(buf, chunk, c):
            v = xT[buf][:, chunk, 0:COLS].rearrange("p (t w c r) -> p t w c r", t=STRIPS, w=NWC, c=WIN_W)
            return v[:, :, :, c, :]

        def xT_psum(chunk, c):
            at = (3 * c + chunk) * PART
            return ps_b16[:, at:at + PART].rearrange("p (t r w) -> p t w r", t=STRIPS, r=WIN_H)

        def oT_tokens(buf, chunk, pair):
            strip, w = 2 * pair // NWC, 2 * pair % NWC
            v = oT[buf][:, chunk, :, :].rearrange("p c (t r w) -> p t w c r", t=STRIPS, r=WIN_H)
            return v[:, strip, w:w + 2, :, :]

        def oT_psum(chunk):
            at = 2 * chunk * TOKE
            return ps_b16[:, at:at + 2 * TOKE].rearrange("p (w n) -> p w n", w=2)[:, :, 0:TOK]\
                .rearrange("p w (c r) -> p w c r", c=WIN_W)

        def scores(row0=0):
            return ps_s[row0:row0 + TOK, :, 0:4 * TOKE].rearrange("p g (a n) -> p g a n", a=4)[:, :, :, 0:TOK]

        def by_window(t, j):
            return t[:, 2 * j * TOKE:2 * (j + 1) * TOKE].rearrange("p (w n) -> p w n", w=2)[:, :, 0:TOK]

        block = ctx.enter_context(nc.Block())

        @block.sync
        def _(sp):
            sp.dma_start(wA[:, :], qkv_w[0:CA, :]).then_inc(dma_w, 16)
            sp.dma_start(wB[0:CB, :], qkv_w[CA:CH, :]).then_inc(dma_w, 16)
            sp.dma_start(wB[CB:128, :], qkv_w[CA:CH, :]).then_inc(dma_w, 16)
            sp.dma_start(pA[:, :], proj_w[0:CA, :]).then_inc(dma_w, 16)
            sp.dma_start(pB[0:CB, :], proj_w[CA:CH, :]).then_inc(dma_w, 16)
            sp.dma_start(pB[CB:128, :], proj_w[CA:CH, :]).then_inc(dma_w, 16)
            v_bias = qkv_b[2 * CH:3 * CH].rearrange("(c a) -> c a", a=1)
            sp.dma_start(bvA[:, :], v_bias[0:CA, :]).then_inc(dma_w, 16)
            sp.dma_start(bvB[:, :], v_bias[CA:CH, :]).then_inc(dma_w, 16)
            sp.dma_start(b_proj[:, :], proj_b.rearrange("(a c) -> a c", a=1)).then_inc(dma_w, 16)
            sp.wait_ge(pool_const, 6)
            qk_bias = qkv_b[0:2 * CH].rearrange("(sj g d) -> g d sj", g=NG, d=HD)
            for g in range(NG):
                sp.dma_start(b_qk[ROW_G * g:ROW_G * g + HD, :], qk_bias[g, :, :],
                             allow_slow_non_contiguous=True).then_inc(dma_bqk, 16)
                sp.dma_start(aug[ROW_G * g:ROW_G * g + HD, 2:4], zeros[ROW_G * g:ROW_G * g + HD, 0:2])\
                    .then_inc(dma_bqk, 16)

            def load_half(b, h, reads):
                reach(sp, stat_read, reads)
                src = x_blk[bass.ds(b * BLOCKS_IMG + 2 * h, 2), :, :].rearrange("s p f -> p s f")
                sp.dma_start(x_stat[h][:, :, :].rearrange("p (s c) d -> p s (c d)", s=2), src)\
                    .then_inc(dma_stat[h], 16)

            for h in range(2):
                load_half(0, h, 0)
            with sp.Fori(1, BATCH) as b:
                reads = sp.snap(b * 2)
                for h in range(2):
                    load_half(b, h, reads + (h - 1))

            def load_x(c, par, count):
                reach(sp, pool_x, count)
                sp.dma_start(x_norm[par][:, :, :].rearrange("p c d -> p (c d)"), x_blk[c, :, :])\
                    .then_inc(dma_x[par], 16)

            def store_y(c, par, rows_done):
                reach(sp, dve_out, rows_done)
                sp.dma_start(out_blk[c, :, :], y_blk[par][:, :, :].rearrange("p c d -> p (c d)"))\
                    .then_inc(dma_out[par], 16)

            def load_y(c, par, stored):
                reach(sp, dma_out[par], stored)
                sp.dma_start(y_blk[par][:, :, :].rearrange("p c d -> p (c d)"), x_blk[c, :, :])\
                    .then_inc(dma_y[par], 16)

            def step(base, blk, c):
                now = base + blk * PAIRS
                par = blk % 2
                if exists(now + 2 * PAIRS):
                    load_x(c + 2, par, now + PAIRS)
                if exists(now - 2 * PAIRS):
                    store_y(c - 2, par, now - PAIRS)
                if exists(now):
                    load_y(c, par, base + (blk // 2) * 16)

            for blk in range(-2, BODY):
                step(0, blk, blk)
            with sp.Fori(1, LAST_IT) as it:
                base = sp.snap(it * SLOTS)
                first = sp.snap(it * BODY)
                for blk in range(BODY):
                    step(base, blk, first + blk)
            for blk in range(BODY + 2):
                step(LAST_IT * SLOTS, blk, LAST_IT * BODY + blk)
            for p in range(2):
                sp.wait_ge(dma_out[p], 16 * (BLOCKS // 2))

        @block.gpsimd
        def _(pool):
            nc.gpsimd.memset(ident[:, :], 0.0).then_inc(pool_const, 1)
            nc.gpsimd.memset(b_qk[:, :], 0.0).then_inc(pool_const, 1)
            nc.gpsimd.memset(zeros[:, :], 0.0).then_inc(pool_const, 1)
            nc.gpsimd.memset(aug[:, 0:2], 0.0).then_inc(pool_const, 1)
            nc.gpsimd.memset(aug[:, 2:4], AUG_ONE).then_inc(pool_const, 1)
            nc.gpsimd.memset(ones[:, :], 1.0).then_inc(pool_const, 1)
            pool.wait_ge(pool_const, 6)
            nc.gpsimd.affine_select(out=ident[:, :], in_=ident[:, :], compare_op=ALU.not_equal, fill=1.0,
                                    base=0, pattern=[[-1, 128]], channel_multiplier=1).then_inc(pool_const, 1)
            pool.wait_ge(weights_big, 1)
            nc.gpsimd.partition_all_reduce(big[:, :], big_own[:, :], 128, RMAX).then_inc(weights_big, 1)
            pool.wait_ge(stats_done, 1)
            pool.wait_ge(setup_done, 1)

            def passed(semaphore, count):
                reach(pool, semaphore, count)
                pool.sem_inc(pool_passed, 1)

            def of_group(table, b, n):
                row = table[:, bass.ds(b * GROUPS, GROUPS)]
                return row.unsqueeze(1).unsqueeze(3).broadcast_to([PART, n, GROUPS, GCH])

            def prepare_x(step, s, b):
                buf = parity(s)
                t0, n = STEP_TILES[s % PAIRS]
                x3, xs = x_norm[buf][:, t0:t0 + n, :], x_split[buf][:, t0:t0 + n, :]
                x4 = x3.rearrange("p c (g k) -> p c g k", k=GCH)
                nc.gpsimd.tensor_tensor(x4, x4, of_group(mean_all, b, n), ALU.subtract).then_inc(pool_x_steps, 1)
                passed(pool_x_steps, step * 3 + 1)
                nc.gpsimd.tensor_tensor(x4, x4, of_group(rstd_all, b, n), ALU.mult).then_inc(pool_x_steps, 1)
                passed(pool_x_steps, step * 3 + 2)
                nc.gpsimd.tensor_copy(xs[:, :, 0:CH], x3).then_inc(pool_x_steps, 1)
                reach(pool, pool_x_steps, step * 3 + 3)
                nc.gpsimd.tensor_tensor(xs[:, :, CH:2 * CA], x3[:, :, CA:CH], xs[:, :, CA:CH], ALU.subtract)
                nc.gpsimd.tensor_tensor(xs[:, :, 2 * CA:3 * CA], x3[:, :, 0:CA], xs[:, :, 0:CA], ALU.subtract)\
                    .then_inc(pool_x, 1)

            def slot(base, s, b_next):
                i = base + s
                if exists(i - O_LAG):
                    reach(pool, act_o, i - O_LAG + 1)
                    nc.gpsimd.tensor_tensor(o_split[:, :, CH:2 * CA], o_sb[:, :, CA:CH], o_split[:, :, CA:CH],
                                            ALU.subtract)
                    nc.gpsimd.tensor_tensor(o_split[:, :, 2 * CA:3 * CA], o_sb[:, :, 0:CA], o_split[:, :, 0:CA],
                                            ALU.subtract).then_inc(pool_o, 1)
                if exists(i - 1):
                    reach(pool, act_exp, i)
                    reach(pool, pe_av, i - 1)
                    nc.gpsimd.tensor_tensor(p_lo[:, 0:16 * TOK], probs[:, :], p_hi[(s - 1) % 2][:, 0:16 * TOK],
                                            ALU.subtract).then_inc(pool_p, 1)
                ahead = (s + PREP_LEAD) // PAIRS
                if exists(i + PREP_LEAD) and (s + PREP_LEAD) % PAIRS == 0:
                    reach(pool, dma_x[ahead % 2], base + 16 * (ahead // 2) + 16)
                    passed(pe_xT, i + PREP_LEAD - PAIRS)
                if exists(i - Y_LAG):
                    r = s - Y_LAG
                    t0, n = STEP_TILES[r % PAIRS]
                    buf = parity(r)
                    if r % PAIRS == 0:
                        reach(pool, dma_y[buf], base + (r // SLOTS) * 16 + 16)
                    y = y_blk[buf][:, t0:t0 + n, :]
                    bias = bias_out[:, :].unsqueeze(1).broadcast_to([PART, n, CH])
                    nc.gpsimd.tensor_tensor(y, y, bias, ALU.add).then_inc(pool_y, 1)
                if exists(i + PREP_LEAD):
                    prepare_x(i + PREP_LEAD, s + PREP_LEAD, b_next(ahead))

            for s in range(-PREP_LEAD, SLOTS):
                slot(0, s, lambda ahead: ahead // BLOCKS_IMG)
            with pool.Fori(1, LAST_IT) as it:
                base = pool.snap(it * SLOTS)
                b_now, b_after = pool.snap(it // 2), pool.snap((it + 1) // 2)
                for s in range(SLOTS):
                    slot(base, s, lambda ahead: b_now if ahead < BODY else b_after)
            for s in range(SLOTS + P_LAG + 1):
                slot(LAST_IT * SLOTS, s, lambda ahead: BATCH - 1)

        @block.scalar
        def _(act):
            act.wait_ge(dve_stat, 2 * BATCH + 1)
            nc.scalar.activation(rstd_all[:, :], var_all[:, :], ACT.Sqrt).then_inc(act_sqrt, 1)
            act.wait_ge(setup_done, 1)

            def slot(base, s):
                i = base + s
                if exists(i - O_LAG):
                    reach(act, dve_norm, i - O_LAG + 1)
                    reach(act, pe_oT, i - O_LAG)
                    nc.scalar.activation(o_split[:, :, 0:CH], o_sb[:, :, :], ACT.Copy).then_inc(act_o, 1)
                if exists(i + 1):
                    k_now, v_now = (s + 1) % 2, (s + 1) % V_BUFS
                    reach(act, pe_v, i + 2)
                    nc.scalar.activation(v_hi[v_now][:, :, 0:HD],
                                         ps_a[0:TOK, 0:2 * CH].rearrange("p (h d) -> p h d", d=HD),
                                         ACT.Copy).then_inc(act_v, 1)
                    reach(act, pe_k, i + 2)
                    for j in range(NJ):
                        last = nc.scalar.activation(by_window(k_hi[k_now], j), by_window(ps_k, j),
                                                    ACT.Identity, bias=b_qk[:, 2 + j:3 + j])
                    last.then_inc(act_k, 1)
                if exists(i + X_LEAD):
                    reach(act, pe_xT, i + X_LEAD + 1)
                    t0, n = STEP_TILES[(s + X_LEAD) % PAIRS]
                    for c in range(n):
                        for chunk in range(3):
                            last = nc.scalar.activation(xT_tokens(parity(s + X_LEAD), chunk, t0 + c),
                                                        xT_psum(chunk, c), ACT.Copy)
                    last.then_inc(act_xT, 1)
                if exists(i):
                    reach(act, pe_scoresT, i + 1)
                    reach(act, pool_p, i)
                    for dst in (probs[:, :], p_hi[s % 2][:, 0:16 * TOK]):
                        last = nc.scalar.activation(dst.rearrange("p (g a n) -> p g a n", g=NG, a=4), scores(),
                                                    ACT.Exp, bias=exp_shift[0:TOK, :], scale=exp_scale[0:TOK, :])
                    last.then_inc(act_exp, 1)
                if exists(i + 1):
                    reach(act, pe_q, i + 2)
                    for j in range(NJ):
                        last = nc.scalar.activation(by_window(q_hi, j), by_window(ps_q, j),
                                                    ACT.Identity, bias=b_qk[:, j:j + 1])
                    last.then_inc(act_q, 1)

            slots(act, slot)

        @block.vector
        def _(dve):
            chained = [0]

            def link(instruction):
                chained[0] += 1
                instruction.then_inc(setup_chain, 1)
                dve.wait_ge(setup_chain, chained[0])

            tt, ts = nc.vector.tensor_tensor, nc.vector.tensor_scalar
            for k in PARTS:
                nc.vector.memset(wqk[k][:, :, :, :], 0.0)
            nc.vector.memset(neg_max[:, :, :, :].bitcast(mybir.dt.uint32), 0)
            nc.vector.memset(exp_shift[:, :], LOG_SHIFT)
            for p in range(V_BUFS):
                nc.vector.memset(v_hi[p][:, :, HD:HD + 1], 1.0)
                nc.vector.memset(v_lo[p][:, :, HD:HD + 1], 0.0)
            for t in (q_hi, q_lo, *k_hi, *k_lo):
                nc.vector.memset(t[:, :], 0.0)
            for t in (p_lo, *p_hi):
                nc.vector.memset(t[:, NG * 4 * TOK:], 0.0)
            for p in range(2):
                last = nc.vector.memset(xT[p][:, :, COLS:], 0.0)
            link(last)
            dve.wait_ge(dma_w, 9 * 16)
            dve.wait_ge(dma_bqk, 2 * NG * 16)
            link(nc.vector.memset(big_parts[:, :, :], 0.0))

            def magnitude(kind, n, t):
                return nc.vector.tensor_reduce(big_parts[:, kind, n:n + 1], t, AXIS.X, ALU.max,
                                               apply_absolute_value=True)

            for kind in range(3):
                magnitude(kind, 0, wA[:, kind * CH:(kind + 1) * CH])
                last = magnitude(kind, 1, wB[:, kind * CH:(kind + 1) * CH])
            magnitude(3, 0, pA[:, :])
            magnitude(3, 1, pB[:, :])
            for kind in range(2):
                last = magnitude(kind, 2, b_qk[:, 2 * kind:2 * kind + 2])
            link(last)
            link(ts(big_parts[:, 0:2, 2:3], big_parts[:, 0:2, 2:3], 1.0 / 64, None, ALU.mult))
            link(nc.vector.tensor_reduce(big_own[:, :], big_parts[:, :, :], AXIS.X, ALU.max))
            link(ts(big_own[:, :], big_own[:, :], 1e-30, None, ALU.max))
            ts(big_own[:, 0:2], big_own[:, 0:2], MARGIN, None, ALU.mult).then_inc(weights_big, 1)
            dve.wait_ge(weights_big, 2)
            link(nc.vector.reciprocal(big_inv[:, :], big[:, :]))
            link(tt(exp_scale[:, :], big[:, 0:1], big[:, 1:2], ALU.mult))
            link(ts(exp_scale[:, :], exp_scale[:, :], float(HD) ** -0.5, None, ALU.mult))
            link(tt(out_scale[:, :], big[:, 2:3], big[:, 3:4], ALU.mult))
            for kind in range(2):
                b2 = b_qk[:, 2 * kind:2 * kind + 2]
                link(nc.vector.scalar_tensor_tensor(out=b2, in0=b2, scalar=big_inv[:, kind:kind + 1],
                                                    in1=aug[:, 2 * kind:2 * kind + 2], op0=ALU.mult, op1=ALU.add))
            nc.vector.tensor_copy(bvA_rep[:, :], bvA[:, 0:1].broadcast_to([CA, PART]))
            nc.vector.tensor_copy(bvB_rep[:, :], bvB[:, 0:1].broadcast_to([CB, PART])).then_inc(setup_w, 1)
            dve.wait_ge(pe_bias, 1)
            link(nc.vector.tensor_copy(bias_out[:, :], ps_a[0:PART, 0:CH]))
            for kind in range(3):
                for w in (wA, wB):
                    part = w[:, kind * CH:(kind + 1) * CH]
                    link(ts(part, part, big_inv[:, kind:kind + 1], None, ALU.mult))
            for w in (pA, pB):
                link(ts(w[:, :], w[:, :], big_inv[:, 3:4], None, ALU.mult))

            def spread(t):
                return t[:, :, :, :].rearrange("p a g e -> p (a g) e")[:, :, 0:HD]

            def heads(w):
                return w[:, 0:2 * CH].rearrange("p (h d) -> p h d", d=HD)

            for src, hi, lo in ((heads(wA), spread(wqk["hiA"]), spread(wqk["loA"])),
                                (heads(wB), spread(wqk["hiB"]), spread(wqk["loB"])),
                                (wA[:, 2 * CH:], wv["hiA"][:, :], wv["loA"][:, :]),
                                (wB[:, 2 * CH:], wv["hiB"][:, :], wv["loB"][:, :]),
                                (pA[:, :], wp["hiA"][:, :], wp["loA"][:, :]),
                                (pB[:, :], wp["hiB"][:, :], wp["loB"][:, :])):
                link(nc.vector.tensor_copy(hi, src))
                link(tt(lo, src, hi, ALU.subtract))
            dve.wait_ge(pool_const, 7)
            link(nc.vector.tensor_copy(ident16[:, :], ident[:, :]))
            ts(ident_aug[:, :], ident[0:TOK, 0:TOKE], 1.0 / AUG_ONE, None, ALU.mult).then_inc(setup_w, 1)

            n_part = HALF * GCH // 2
            mean_v = stat6[:, :, :, :].rearrange("p h g (e t) -> p h g e t", e=2)[:, :, :, :, 1]
            m2_v = stat6[:, :, :, :].rearrange("p h g (e t) -> p h g e t", e=2)[:, :, :, :, 2]
            STEPS = 6

            def stats_of(b):
                done = [0]

                def step(instruction):
                    done[0] += 1
                    instruction.then_inc(stats_chain, 1)
                    dve.wait_ge(stats_chain, b * STEPS + done[0])

                for h in range(2):
                    dve.wait_ge(dma_stat[h], b * 16 + 16)
                    for g in range(GROUPS):
                        last = nc.vector.bn_stats(stat6[:, h, g, :], x_stat[h][:, :, GCH * g:GCH * (g + 1)])
                    last.then_inc(stat_read, 1)
                dve.wait_ge(pe_stat, b * 2 + 1)
                step(nc.vector.tensor_reduce(st_sum[:, :], stat_sum_view(), AXIS.XY, ALU.add))
                mean_b = mean_all[:, bass.ds(b * GROUPS, GROUPS)]
                step(ts(mean_b, st_sum[:, :], 1.0 / (4 * PART), None, ALU.mult))
                step(tt(st_dev[:, :, :, :], mean_v,
                        mean_b.unsqueeze(1).unsqueeze(3).broadcast_to([PART, 2, GROUPS, 2]), ALU.subtract))
                step(tt(st_sq[:, :, :, :], st_dev[:, :, :, :], st_dev[:, :, :, :], ALU.mult))
                nc.vector.scalar_tensor_tensor(out=st_dev[:, :, :, :], in0=st_sq[:, :, :, :], scalar=float(n_part),
                                               in1=m2_v, op0=ALU.mult, op1=ALU.add).then_inc(dve_stat, 2)
                dve.wait_ge(pe_stat, b * 2 + 2)
                step(nc.vector.tensor_reduce(st_sum[:, :], stat_sum_view(), AXIS.XY, ALU.add))
                step(ts(var_all[:, bass.ds(b * GROUPS, GROUPS)], st_sum[:, :], 1.0 / (4 * PART * n_part), EPS,
                        ALU.mult, ALU.add))

            def stat_sum_view():
                return ps_b[0:PART, 0:4 * GROUPS].rearrange("p (h g e) -> p g h e", h=2, g=GROUPS)

            with dve.Fori(0, BATCH) as b:
                stats_of(b)
            nc.vector.nop().then_inc(dve_stat, 1)
            dve.wait_ge(act_sqrt, 1)
            link(nc.vector.reciprocal(rstd_all[:, :], rstd_all[:, :]))
            link(tt(newton[:, :], rstd_all[:, :], rstd_all[:, :], ALU.mult))
            link(tt(newton[:, :], newton[:, :], var_all[:, :], ALU.mult))
            link(ts(newton[:, :], newton[:, :], -0.5, 1.5, ALU.mult, ALU.add))
            tt(rstd_all[:, :], rstd_all[:, :], newton[:, :], ALU.mult).then_inc(stats_done, 1)
            nc.vector.nop().then_inc(setup_done, 1)

            def lo_part(dst, psum, hi, bias=None):
                if bias is None:
                    return tt(dst, psum, hi, ALU.subtract)
                return nc.vector.scalar_tensor_tensor(out=dst, in0=psum, scalar=bias, in1=hi,
                                                      op0=ALU.add, op1=ALU.subtract)

            def slot(base, s):
                i = base + s
                if exists(i - 1 - P_LAG):
                    r = s - 1 - P_LAG
                    t0, n = STEP_TILES[r % PAIRS]
                    reach(dve, pe_proj, i - P_LAG)
                    reach(dve, pool_y, i - P_LAG)
                    y = y_blk[parity(r)][:, t0:t0 + n, :]
                    nc.vector.scalar_tensor_tensor(
                        out=y, in0=ps_b[0:PART, 0:n * CH].rearrange("p (c d) -> p c d", d=CH),
                        scalar=out_scale[0:PART, :], in1=y, op0=ALU.mult, op1=ALU.add).then_inc(dve_out, 1)
                if exists(i):
                    reach(dve, pe_scores, i + 1)
                    nc.vector.tensor_reduce(neg_max[:, :, :, HD:HD + 1].rearrange("p a g e -> p g (a e)"),
                                            scores(), AXIS.X, ALU.max, negate=True).then_inc(dve_max, 1)
                if exists(i + 1):
                    v_now = (s + 1) % V_BUFS
                    reach(dve, act_v, i + 2)
                    lo_part(v_lo[v_now][:, :, 0:HD], ps_a[0:TOK, 0:2 * CH].rearrange("p (h d) -> p h d", d=HD),
                            v_hi[v_now][:, :, 0:HD]).then_inc(dve_v, 1)
                if exists(i):
                    reach(dve, pe_max, i + 1)
                    for j in range(NJ):
                        last = lo_part(by_window(q_lo, j), by_window(ps_q, j), by_window(q_hi, j), b_qk[:, j:j + 1])
                    last.then_inc(dve_q, 1)
                if exists(i + 1):
                    reach(dve, act_k, i + 2)
                    k_now = (s + 1) % 2
                    for j in range(NJ):
                        last = lo_part(by_window(k_lo[k_now], j), by_window(ps_k, j), by_window(k_hi[k_now], j),
                                       b_qk[:, 2 + j:3 + j])
                    last.then_inc(dve_k, 1)
                if exists(i - O_LAG):
                    o = s - O_LAG
                    reach(dve, pe_oT, i - O_LAG + 1)
                    for chunk in range(3):
                        last = nc.vector.tensor_copy(oT_tokens(parity(o), chunk, o % PAIRS), oT_psum(chunk))
                    last.then_inc(dve_oT, 1)
                if exists(i - 1):
                    reach(dve, pe_av, i)
                    reach(dve, pool_o, i - 1)
                    av = ps_a[0:TOK, 0:2 * HEADS * (HD + 1)].rearrange("p (h e) -> p h e", e=HD + 1)
                    nc.vector.reciprocal(recip[:, :, :], av[:, :, HD:HD + 1]).then_inc(dve_recip, 1)
                    reach(dve, dve_recip, i)
                    tt(o_sb[:, :, :].rearrange("p w (h d) -> p (w h) d", d=HD), av[:, :, 0:HD],
                       recip[:, :, :].broadcast_to([TOK, 2 * HEADS, HD]), ALU.mult).then_inc(dve_norm, 1)

            slots(dve, slot)

        @block.tensor
        def _(pe):
            mm = nc.tensor.matmul
            pe.wait_ge(setup_w, 1)
            mm(ps_a[0:PART, 0:CH], bvA_rep[:, :], pA[:, :], start=True, stop=False)
            mm(ps_a[0:PART, 0:CH], bvB_rep[:, :], pB[0:CB, :], start=False, stop=False)
            mm(ps_a[0:PART, 0:CH], ones[0:1, :], b_proj[:, :], start=False, stop=True).then_inc(pe_bias, 1)

            mean_v = stat6[:, :, :, :].rearrange("p h g (e t) -> p (h g) e t", e=2)[:, :, :, 1]
            with pe.Fori(0, BATCH) as b:
                pe.wait_ge(stat_read, b * 2 + 2)
                mm(ps_b[0:PART, 0:4 * GROUPS].rearrange("p (a e) -> p a e", e=2), ones[0:PART, :], mean_v,
                   start=True, stop=True).then_inc(pe_stat, 1)
                pe.wait_ge(dve_stat, b * 2 + 2)
                mm(ps_b[0:PART, 0:4 * GROUPS], ones[0:PART, :],
                   st_dev[:, :, :, :].rearrange("p h g e -> p (h g e)"), start=True, stop=True).then_inc(pe_stat, 1)
            pe.wait_ge(setup_w, 2)
            pe.wait_ge(setup_done, 1)

            def products(dst, pairs, first=True, closes=True):
                for n, (lhsT, rhs) in enumerate(pairs):
                    last = mm(dst, lhsT, rhs, start=first and n == 0, stop=closes and n == len(pairs) - 1,
                              skip_group_check=True)
                return last

            def chunks(t, w, rows_are_tokens):
                both = ((t[:, A_HI, :], w["hiA"]), (t[:, A_HI, :], w["loA"]), (t[:, A_LO, :], w["hiA"]),
                        (t[:, B_BOTH, :], w["hiB"]), (t[0:CB, B_BOTH, :], w["loB"][0:CB, :]))
                return both if rows_are_tokens else tuple((b, a) for a, b in both)

            def qk_projection(bank, which, s, semaphore):
                at = 2 * (s % PAIRS) * TOK
                tokens = xT[parity(s)][:, :, at:at + 2 * TOK]
                for j in range(NJ):
                    w = {k: wqk[k][:, 2 * which + j, :, :].rearrange("p g e -> p (g e)") for k in PARTS}
                    last = products(by_window(bank, j), chunks(tokens, w, False), first=j == 0)
                last.then_inc(semaphore, 1)

            def rows(g):
                return slice(ROW_G * g, ROW_G * g + AUG)

            def slot(base, s):
                i = base + s
                kb = s % 2
                if exists(i):
                    reach(pe, act_q, i + 1)
                    reach(pe, act_k, i + 1)
                    reach(pe, act_exp, i)
                    for w in range(2):
                        for j in range(NJ):
                            a, at = (2 * j + w) * TOKE, (2 * w + j) * TOKE
                            for g in range(NG):
                                last = mm(ps_s[:, g, at:at + TOK], q_hi[rows(g), a:a + FULL],
                                          k_hi[kb][rows(g), a:a + TOK], start=True, stop=True)
                    last.then_inc(pe_scores, 1)
                if exists(i + 1):
                    if (s + 1) % PAIRS == 0:
                        reach(pe, act_xT, i + 1 + PAIRS)
                    reach(pe, dve_norm, i - 1)
                    if not exists(i - 2):
                        reach(pe, dve_v, i + 1)
                    buf, pair = parity(s + 1), (s + 1) % PAIRS
                    for w in range(2):
                        at = (2 * pair + w) * TOK
                        weights = {k: wv[k][:, :] for k in PARTS}
                        last = products(ps_a[:, w * CH:(w + 1) * CH],
                                        chunks(xT[buf][:, :, at:at + FULL], weights, True))
                    last.then_inc(pe_v, 1)
                    reach(pe, dve_k, i + 1)
                    qk_projection(ps_k, 1, s + 1, pe_k)
                if exists(i):
                    reach(pe, dve_max, i + 1)
                    for w in range(2):
                        for j in range(NJ):
                            at = (2 * j + w) * TOKE
                            last = mm(ps_q[:, at:at + TOKE],
                                      neg_max[:, 2 * w + j, :, :].rearrange("p g e -> p (g e)"), ident_aug[:, :],
                                      start=False, stop=True, skip_group_check=True)
                    last.then_inc(pe_max, 1)
                if exists(i + X_LEAD):
                    reach(pe, dve_out, i - 1 - P_LAG + 1)
                    if not exists(i - 1 - P_LAG):
                        reach(pe, act_xT, i + X_LEAD)
                    x_step = s + X_LEAD
                    reach(pe, pool_x, i + X_LEAD + 1)
                    t0, n = STEP_TILES[x_step % PAIRS]
                    for c in range(n):
                        for chunk in range(3):
                            at = (3 * c + chunk) * PART
                            last = nc.tensor.transpose(ps_b16[:, at:at + PART],
                                                       x_split[parity(x_step)][:, t0 + c, chunk * 128:(chunk + 1) * 128],
                                                       ident16[0:PART, 0:PART])
                    last.then_inc(pe_xT, 1)
                if exists(i):
                    reach(pe, dve_q, i + 1)
                    for w in range(2):
                        for j in range(NJ):
                            a, at = (2 * j + w) * TOKE, (2 * w + j) * TOKE
                            for n, (k, q) in enumerate(((k_hi[kb], q_hi), (k_lo[kb], q_hi), (k_hi[kb], q_lo))):
                                for g in range(NG):
                                    last = mm(ps_s[:, g, at:at + TOK], k[rows(g), a:a + FULL], q[rows(g), a:a + TOK],
                                              start=n == 0, stop=n == 2)
                    last.then_inc(pe_scoresT, 1)
                if exists(i - O_LAG):
                    reach(pe, pool_o, i - O_LAG + 1)
                    reach(pe, act_xT, min(i + X_LEAD + 1, N_PAIRS) if isinstance(i, int) else i + X_LEAD + 1)
                    if not exists(i + X_LEAD):
                        reach(pe, dve_out, i - 1 - P_LAG + 1)
                    for chunk in range(3):
                        for w in range(2):
                            at = (2 * chunk + w) * TOKE
                            last = nc.tensor.transpose(ps_b16[:, at:at + TOK],
                                                       o_split[:, w, chunk * 128:(chunk + 1) * 128],
                                                       ident16[0:TOK, 0:TOK])
                    last.then_inc(pe_oT, 1)
                if exists(i - 1):
                    reach(pe, pool_p, i)
                    reach(pe, dve_v, (i + 2) if exists(i + 1) else i)
                    v_now = (s - 1) % V_BUFS
                    for w in range(2):
                        for j in range(NJ):
                            for g in range(NG):
                                h, at = HEADS * w + NG * j + g, (4 * g + 2 * w + j) * TOK
                                last = products(ps_a[:, h * (HD + 1):(h + 1) * (HD + 1)], (
                                    (p_hi[(s - 1) % 2][:, at:at + FULL], v_hi[v_now][:, h, :]),
                                    (p_hi[(s - 1) % 2][:, at:at + FULL], v_lo[v_now][:, h, :]),
                                    (p_lo[:, at:at + FULL], v_hi[v_now][:, h, :])))
                    last.then_inc(pe_av, 1)
                if exists(i + 1):
                    reach(pe, dve_q, i + 1)
                    qk_projection(ps_q, 0, s + 1, pe_q)
                if exists(i - P_LAG):
                    reach(pe, dve_oT, min(i - O_LAG + 1, N_PAIRS) if isinstance(i, int) else i - O_LAG + 1)
                    if not exists(i - O_LAG):
                        reach(pe, dve_out, i - P_LAG)
                    r = s - P_LAG
                    t0, n = STEP_TILES[r % PAIRS]
                    for c in range(n):
                        weights = {k: wp[k][:, :] for k in PARTS}
                        last = products(ps_b[0:PART, c * CH:(c + 1) * CH],
                                        chunks(oT[parity(r)][:, :, t0 + c, :], weights, True))
                    last.then_inc(pe_proj, 1)

            slots(pe, slot)


def kernel(x, L0_conv_qkv_w, L0_conv_qkv_b, L0_conv_proj_w, L0_conv_proj_b):
    import numpy as np
    import concourse.bacc as bacc
    from concourse.bass_utils import run_bass_kernel_spmd

    nc = bacc.Bacc("TRN2", target_bir_lowering=False, num_devices=1)
    given = {"x": x, "qkv_w": L0_conv_qkv_w, "qkv_b": L0_conv_qkv_b, "proj_w": L0_conv_proj_w, "proj_b": L0_conv_proj_b}
    arrays = {f"in_{name}": np.ascontiguousarray(a) for name, a in given.items()}
    args = [nc.dram_tensor(name, a.shape, mybir.dt.from_np(a.dtype), kind="ExternalInput").ap()
            for name, a in arrays.items()]
    out = nc.dram_tensor("out", (BATCH, HEIGHT, WIDTH, CH), F32, kind="ExternalOutput").ap()
    window_attention(nc, *args, out)
    result = run_bass_kernel_spmd(nc, [arrays], core_ids=[0])
    return result.results[0]["out"]
```

```python
import math
from contextlib import ExitStack

import concourse.bass as bass
from concourse import mybir

F32 = mybir.dt.float32
F32R = mybir.dt.float32r
F16 = mybir.dt.float16
ALU = mybir.AluOpType
ACT = mybir.ActivationFunctionType
AXIS = mybir.AxisListType
RMAX = bass.bass_isa.ReduceOp.max

BATCH, HEIGHT, WIDTH, CH = 8, 56, 88, 192
WIN_H, WIN_W = 7, 11
TOK = WIN_H * WIN_W
TOKE = TOK + 1
HEADS, HD = 8, 24
GROUPS, GCH = 32, 6
EPS = 1e-5
NWC = WIDTH // WIN_W
STRIPS = 2
ROWS = STRIPS * WIN_H
PART = ROWS * NWC
BLOCKS = BATCH * HEIGHT // ROWS
BLOCKS_IMG = HEIGHT // ROWS
WINS = STRIPS * NWC
PAIRS = WINS // 2
N_PAIRS = BLOCKS * PAIRS
TILES = WIN_W
COLS = WINS * TOK
CA, CB = 128, CH - 128
ROW_G, NG, NJ = 32, 4, 2
AUG = HD + 1
STEP_TILES = [(0, 2), (2, 2), (4, 2), (6, 1), (7, 1), (8, 1), (9, 1), (10, 1)]
BODY = 2
SLOTS = BODY * PAIRS
LAST_IT = BLOCKS // BODY - 1
NORM_LEAD = PAIRS + 3
SPLIT_LEAD = PAIRS + 2
X_LEAD = PAIRS + 1
AV_LAG = 2
O_LAG = AV_LAG + 1
T_LAG = O_LAG + 1
P_LAG = PAIRS + O_LAG
Y_LAG = PAIRS - 1
V_BUFS = 4
FULL = 128
PAD = FULL - TOK
AUG_ONE = 32768.0
MARGIN = 4.0
LOG_SHIFT = math.log(64.0)
A_HI, B_BOTH, A_LO = range(3)


def window_attention(nc, x, qkv_w, qkv_b, proj_w, proj_b, out):
    x_blk = x.rearrange("b (s r) (w c) d -> (b s) (r w) (c d)", r=ROWS, c=WIN_W)
    out_blk = out.rearrange("b (s r) (w c) d -> (b s) (r w) (c d)", r=ROWS, c=WIN_W)

    with ExitStack() as ctx:
        def sb(name, shape, dt=F32):
            return ctx.enter_context(nc.sbuf_tensor(name, shape, dt))

        def sem(name):
            return ctx.enter_context(nc.semaphore(name))

        ident = sb("ident", [128, 128])
        ident16 = sb("ident16", [128, 128], F16)
        ident_aug = sb("ident_aug", [TOK, TOKE], F32R)
        ones = sb("ones", [128, PART])
        wA, wB = sb("wA", [CA, 3 * CH]), sb("wB", [128, 3 * CH])
        pA, pB = sb("pA", [CA, CH]), sb("pB", [128, CH])
        PARTS = ("hiA", "loA", "hiB", "loB")
        wqk = {k: sb(f"wqk_{k}", [128, 4, NG, ROW_G], F16) for k in PARTS}
        wv = {k: sb(f"wv_{k}", [128, CH], F16) for k in PARTS}
        wp = {k: sb(f"wp_{k}", [128, CH], F16) for k in PARTS}
        b_qk, aug, zeros = sb("b_qk", [128, 4]), sb("aug", [128, 4]), sb("zeros", [128, 4])
        bvA, bvB, b_proj = sb("bvA", [CA, 1]), sb("bvB", [CB, 1]), sb("b_proj", [1, CH])
        bvA_rep, bvB_rep = sb("bvA_rep", [CA, PART]), sb("bvB_rep", [CB, PART])
        bias_out = sb("bias_out", [PART, CH])
        big_parts, big_own, big = sb("big_parts", [128, 4, 3]), sb("big_own", [128, 4]), sb("big", [128, 4])
        big_inv = sb("big_inv", [128, 4])
        exp_scale, out_scale, exp_shift = sb("exp_scale", [128, 1]), sb("out_scale", [128, 1]), sb("exp_shift", [128, 1])
        HALF = 2 * WIN_W
        x_stat = [sb(f"x_stat{h}", [PART, HALF, CH]) for h in range(2)]
        stat6 = sb("stat6", [PART, BATCH, 2, GROUPS, 6])
        mean_all, var_all = sb("mean_all", [PART, BATCH * GROUPS]), sb("var_all", [PART, BATCH * GROUPS])
        rstd_all, newton = sb("rstd_all", [PART, BATCH * GROUPS]), sb("newton", [PART, BATCH * GROUPS])
        st_dev = sb("st_dev", [PART, BATCH, 2, GROUPS, 2])
        st_sq = sb("st_sq", [PART, BATCH, 2, GROUPS, 2])
        st_sum = sb("st_sum", [PART, BATCH * GROUPS])
        x_norm = [sb(f"x_norm{p}", [PART, TILES, CH]) for p in range(2)]
        x_split = [sb(f"x_split{p}", [PART, TILES, 2 * CH], F16) for p in range(2)]
        y_blk = [sb(f"y_blk{p}", [PART, TILES, CH]) for p in range(2)]
        xT = [sb(f"xT{p}", [128, 3, COLS + PAD], F16) for p in range(2)]
        oT = [sb(f"oT{p}", [128, 3, TILES, PART], F16) for p in range(2)]
        def sb_qk(name):
            return sb(name, [128, 4 * TOKE + PAD], F16)

        q_hi, q_lo = sb_qk("q_hi"), sb_qk("q_lo")
        k_hi = [sb_qk(f"k_hi{p}") for p in range(2)]
        k_lo = [sb_qk(f"k_lo{p}") for p in range(2)]
        v_hi = [sb(f"v_hi{p}", [TOK, 2 * HEADS, HD + 1], F16) for p in range(V_BUFS)]
        v_lo = [sb(f"v_lo{p}", [TOK, 2 * HEADS, HD + 1], F16) for p in range(V_BUFS)]
        neg_max = sb("neg_max", [TOK, 4, NG, ROW_G], F32R)
        probs = sb("probs", [TOK, NG * 4 * TOK])
        p_hi = [sb(f"p_hi{p}", [TOK, NG * 4 * TOK + PAD], F16) for p in range(2)]
        p_lo = [sb(f"p_lo{p}", [TOK, NG * 4 * TOK + PAD], F16) for p in range(2)]
        recip = sb("recip", [TOK, 2 * HEADS, 1])
        o_sb = [sb(f"o_sb{p}", [TOK, 2, CH]) for p in range(2)]
        o_split = sb("o_split", [TOK, 2, 2 * CH], F16)
        ps_s = ctx.enter_context(nc.psum_tensor("ps_s", [128, NG, 512], F32))
        ps_q = ctx.enter_context(nc.psum_tensor("ps_q", [128, 512], F32))
        ps_k = ctx.enter_context(nc.psum_tensor("ps_k", [128, 512], F32))
        ps_a = ctx.enter_context(nc.psum_tensor("ps_a", [128, 512], F32))
        ps_b = ctx.enter_context(nc.psum_tensor("ps_b", [128, 512], F32))
        ps_b16 = ps_b[:, :].bitcast(F16)

        pe_scores, pe_scoresT, pe_max = sem("pe_scores"), sem("pe_scoresT"), sem("pe_max_added")
        pe_q, pe_k, pe_v = sem("pe_q"), sem("pe_k"), sem("pe_v")
        pe_av, pe_oT, pe_proj, pe_xT = sem("pe_av"), sem("pe_oT"), sem("pe_proj"), sem("pe_xT")
        act_k, act_exp, act_xT = sem("act_k"), sem("act_exp"), sem("act_xT")
        act_p, act_o, act_oT, act_x = sem("act_p"), sem("act_o"), sem("act_oT"), sem("act_x")
        dve_max, dve_q_hi, dve_q = sem("dve_max"), sem("dve_q_hi"), sem("dve_q")
        dve_k, dve_v_hi, dve_v = sem("dve_k"), sem("dve_v_hi"), sem("dve_v")
        dve_norm, dve_recip = sem("dve_norm"), sem("dve_recip")
        dve_out = sem("dve_out")
        pool_p, pool_o, pool_x, pool_y = sem("pool_p"), sem("pool_o"), sem("pool_x"), sem("pool_y")
        dma_x = [sem(f"dma_x{p}") for p in range(2)]
        dma_y = [sem(f"dma_y{p}") for p in range(2)]
        dma_out = [sem(f"dma_out{p}") for p in range(2)]
        pool_centred, pool_norm, pool_passed = sem("pool_centred"), sem("pool_norm"), sem("pool_passed")
        dma_w, dma_bqk, dma_stat = sem("dma_w"), sem("dma_bqk"), [sem("dma_stat0"), sem("dma_stat1")]
        pool_const, setup_w = sem("pool_const"), sem("setup_w")
        weights_big = sem("weights_big")
        dve_stat, pe_stat, setup_chain = sem("dve_stat"), sem("pe_stat"), sem("setup_chain")
        act_sqrt, stats_done, stat_read = sem("act_sqrt"), sem("stats_done"), sem("stat_read")
        pe_bias, setup_done = sem("pe_bias"), sem("setup_done")

        def reach(eng, semaphore, count):
            if isinstance(count, int) and count <= 0:
                return
            eng.wait_ge(semaphore, count)

        def exists(index, limit=N_PAIRS):
            return not isinstance(index, int) or 0 <= index < limit

        def parity(s):
            return (s // PAIRS) % 2

        def slots(eng, slot):
            for s in range(-NORM_LEAD, SLOTS):
                slot(0, s)
            with eng.Fori(1, LAST_IT) as it:
                base = eng.snap(it * SLOTS)
                for s in range(SLOTS):
                    slot(base, s)
            for s in range(SLOTS + P_LAG):
                slot(LAST_IT * SLOTS, s)

        def x_step(bufs, s):
            t0, n = STEP_TILES[s % PAIRS]
            return bufs[parity(s)][:, t0:t0 + n, :]

        def xT_tokens(buf, chunk, c):
            v = xT[buf][:, chunk, 0:COLS].rearrange("p (t w c r) -> p t w c r", t=STRIPS, w=NWC, c=WIN_W)
            return v[:, :, :, c, :]

        def xT_psum(chunk, c):
            at = (3 * c + chunk) * PART
            return ps_b16[:, at:at + PART].rearrange("p (t r w) -> p t w r", t=STRIPS, r=WIN_H)

        def oT_tokens(buf, chunk, pair):
            strip, w = 2 * pair // NWC, 2 * pair % NWC
            v = oT[buf][:, chunk, :, :].rearrange("p c (t r w) -> p t w c r", t=STRIPS, r=WIN_H)
            return v[:, strip, w:w + 2, :, :]

        def oT_psum(chunk):
            at = 2 * chunk * TOKE
            return ps_b16[:, at:at + 2 * TOKE].rearrange("p (w n) -> p w n", w=2)[:, :, 0:TOK]\
                .rearrange("p w (c r) -> p w c r", c=WIN_W)

        def scores(row0=0):
            return ps_s[row0:row0 + TOK, :, 0:4 * TOKE].rearrange("p g (a n) -> p g a n", a=4)[:, :, :, 0:TOK]

        def by_window(t, j):
            return t[:, 2 * j * TOKE:2 * (j + 1) * TOKE].rearrange("p (w n) -> p w n", w=2)[:, :, 0:TOK]

        block = ctx.enter_context(nc.Block())

        @block.sync
        def _(sp):
            sp.dma_start(wA[:, :], qkv_w[0:CA, :]).then_inc(dma_w, 16)
            sp.dma_start(wB[0:CB, :], qkv_w[CA:CH, :]).then_inc(dma_w, 16)
            sp.dma_start(wB[CB:128, :], qkv_w[CA:CH, :]).then_inc(dma_w, 16)
            sp.dma_start(pA[:, :], proj_w[0:CA, :]).then_inc(dma_w, 16)
            sp.dma_start(pB[0:CB, :], proj_w[CA:CH, :]).then_inc(dma_w, 16)
            sp.dma_start(pB[CB:128, :], proj_w[CA:CH, :]).then_inc(dma_w, 16)
            v_bias = qkv_b[2 * CH:3 * CH].rearrange("(c a) -> c a", a=1)
            sp.dma_start(bvA[:, :], v_bias[0:CA, :]).then_inc(dma_w, 16)
            sp.dma_start(bvB[:, :], v_bias[CA:CH, :]).then_inc(dma_w, 16)
            sp.dma_start(b_proj[:, :], proj_b.rearrange("(a c) -> a c", a=1)).then_inc(dma_w, 16)
            sp.wait_ge(pool_const, 6)
            qk_bias = qkv_b[0:2 * CH].rearrange("(sj g d) -> g d sj", g=NG, d=HD)
            for g in range(NG):
                sp.dma_start(b_qk[ROW_G * g:ROW_G * g + HD, :], qk_bias[g, :, :],
                             allow_slow_non_contiguous=True).then_inc(dma_bqk, 16)
                sp.dma_start(aug[ROW_G * g:ROW_G * g + HD, 2:4], zeros[ROW_G * g:ROW_G * g + HD, 0:2])\
                    .then_inc(dma_bqk, 16)

            def load_half(b, h, reads):
                reach(sp, stat_read, reads)
                src = x_blk[bass.ds(b * BLOCKS_IMG + 2 * h, 2), :, :].rearrange("s p f -> p s f")
                sp.dma_start(x_stat[h][:, :, :].rearrange("p (s c) d -> p s (c d)", s=2), src)\
                    .then_inc(dma_stat[h], 16)

            for h in range(2):
                load_half(0, h, 0)
            with sp.Fori(1, BATCH) as b:
                reads = sp.snap(b * 2)
                for h in range(2):
                    load_half(b, h, reads + (h - 1))

            def load_x(c, par, count):
                reach(sp, pool_x, count)
                sp.dma_start(x_norm[par][:, :, :].rearrange("p c d -> p (c d)"), x_blk[c, :, :])\
                    .then_inc(dma_x[par], 16)

            def store_y(c, par, rows_done):
                reach(sp, dve_out, rows_done)
                sp.dma_start(out_blk[c, :, :], y_blk[par][:, :, :].rearrange("p c d -> p (c d)"))\
                    .then_inc(dma_out[par], 16)

            def load_y(c, par, stored):
                reach(sp, dma_out[par], stored)
                sp.dma_start(y_blk[par][:, :, :].rearrange("p c d -> p (c d)"), x_blk[c, :, :])\
                    .then_inc(dma_y[par], 16)

            def step(base, blk, c):
                now = base + blk * PAIRS
                par = blk % 2
                if exists(now + 2 * PAIRS):
                    load_x(c + 2, par, now + PAIRS)
                if exists(now - 2 * PAIRS):
                    store_y(c - 2, par, now - PAIRS)
                if exists(now):
                    load_y(c, par, base + (blk // 2) * 16)

            for blk in range(-2, BODY):
                step(0, blk, blk)
            with sp.Fori(1, LAST_IT) as it:
                base = sp.snap(it * SLOTS)
                first = sp.snap(it * BODY)
                for blk in range(BODY):
                    step(base, blk, first + blk)
            for blk in range(BODY + 2):
                step(LAST_IT * SLOTS, blk, LAST_IT * BODY + blk)
            for p in range(2):
                sp.wait_ge(dma_out[p], 16 * (BLOCKS // 2))

        @block.gpsimd
        def _(pool):
            nc.gpsimd.memset(ident[:, :], 0.0).then_inc(pool_const, 1)
            nc.gpsimd.memset(b_qk[:, :], 0.0).then_inc(pool_const, 1)
            nc.gpsimd.memset(zeros[:, :], 0.0).then_inc(pool_const, 1)
            nc.gpsimd.memset(aug[:, 0:2], 0.0).then_inc(pool_const, 1)
            nc.gpsimd.memset(aug[:, 2:4], AUG_ONE).then_inc(pool_const, 1)
            nc.gpsimd.memset(ones[:, :], 1.0).then_inc(pool_const, 1)
            pool.wait_ge(pool_const, 6)
            nc.gpsimd.affine_select(out=ident[:, :], in_=ident[:, :], compare_op=ALU.not_equal, fill=1.0,
                                    base=0, pattern=[[-1, 128]], channel_multiplier=1).then_inc(pool_const, 1)
            pool.wait_ge(weights_big, 1)
            nc.gpsimd.partition_all_reduce(big[:, :], big_own[:, :], 128, RMAX).then_inc(weights_big, 1)
            pool.wait_ge(stats_done, 1)
            pool.wait_ge(setup_done, 1)

            def passed(semaphore, count):
                reach(pool, semaphore, count)
                pool.sem_inc(pool_passed, 1)

            def of_group(table, b, n):
                row = table[:, bass.ds(b * GROUPS, GROUPS)]
                return row.unsqueeze(1).unsqueeze(3).broadcast_to([PART, n, GROUPS, GCH])

            def slot(base, s, image):
                i = base + s
                if exists(i - 1):
                    reach(pool, act_p, i)
                    reach(pool, pe_av, i - 2)
                    nc.gpsimd.tensor_tensor(p_lo[(s - 1) % 2][:, 0:16 * TOK], probs[:, :], p_hi[(s - 1) % 2][:, 0:16 * TOK],
                                            ALU.subtract).then_inc(pool_p, 1)
                if exists(i - O_LAG):
                    reach(pool, act_o, i - O_LAG + 1)
                    o = o_sb[(s - O_LAG) % 2]
                    nc.gpsimd.tensor_tensor(o_split[:, :, CH:2 * CA], o[:, :, CA:CH], o_split[:, :, CA:CH],
                                            ALU.subtract)
                    nc.gpsimd.tensor_tensor(o_split[:, :, 2 * CA:3 * CA], o[:, :, 0:CA], o_split[:, :, 0:CA],
                                            ALU.subtract).then_inc(pool_o, 1)
                if exists(i + SPLIT_LEAD):
                    reach(pool, act_x, i + SPLIT_LEAD + 1)
                    x3, xs = x_step(x_norm, s + SPLIT_LEAD), x_step(x_split, s + SPLIT_LEAD)
                    nc.gpsimd.tensor_tensor(xs[:, :, CH:2 * CA], x3[:, :, CA:CH], xs[:, :, CA:CH], ALU.subtract)
                    nc.gpsimd.tensor_tensor(xs[:, :, 2 * CA:3 * CA], x3[:, :, 0:CA], xs[:, :, 0:CA], ALU.subtract)\
                        .then_inc(pool_x, 1)
                ahead = (s + NORM_LEAD) // PAIRS
                if exists(i + NORM_LEAD) and (s + NORM_LEAD) % PAIRS == 0:
                    reach(pool, dma_x[ahead % 2], base + 16 * (ahead // 2) + 16)
                if exists(i - Y_LAG):
                    r = s - Y_LAG
                    if r % PAIRS == 0:
                        reach(pool, dma_y[parity(r)], base + (r // SLOTS) * 16 + 16)
                    y = x_step(y_blk, r)
                    bias = bias_out[:, :].unsqueeze(1).broadcast_to([PART, STEP_TILES[r % PAIRS][1], CH])
                    nc.gpsimd.tensor_tensor(y, y, bias, ALU.add).then_inc(pool_y, 1)
                if exists(i + NORM_LEAD):
                    n = STEP_TILES[(s + NORM_LEAD) % PAIRS][1]
                    x4 = x_step(x_norm, s + NORM_LEAD).rearrange("p c (g k) -> p c g k", k=GCH)
                    b = image(ahead)
                    nc.gpsimd.tensor_tensor(x4, x4, of_group(mean_all, b, n), ALU.subtract).then_inc(pool_centred, 1)
                    passed(pool_centred, i + NORM_LEAD + 1)
                    nc.gpsimd.tensor_tensor(x4, x4, of_group(rstd_all, b, n), ALU.mult).then_inc(pool_norm, 1)

            for s in range(-NORM_LEAD, SLOTS):
                slot(0, s, lambda ahead: ahead // BLOCKS_IMG)
            with pool.Fori(1, LAST_IT) as it:
                base = pool.snap(it * SLOTS)
                b_now, b_after = pool.snap(it // 2), pool.snap((it + 1) // 2)
                for s in range(SLOTS):
                    slot(base, s, lambda ahead: b_now if ahead < BODY else b_after)
            for s in range(SLOTS + P_LAG):
                slot(LAST_IT * SLOTS, s, lambda ahead: BATCH - 1)

        @block.scalar
        def _(act):
            act.wait_ge(dve_stat, 2)
            nc.scalar.activation(rstd_all[:, :], var_all[:, :], ACT.Sqrt).then_inc(act_sqrt, 1)
            act.wait_ge(setup_done, 1)

            def slot(base, s):
                i = base + s
                if exists(i - 1):
                    reach(act, act_exp, i)
                    reach(act, pe_av, i - 2)
                    nc.scalar.activation(p_hi[(s - 1) % 2][:, 0:16 * TOK], probs[:, :], ACT.Copy).then_inc(act_p, 1)
                if exists(i - T_LAG):
                    o = s - T_LAG
                    reach(act, pe_oT, i - T_LAG + 1)
                    for chunk in range(3):
                        last = nc.scalar.activation(oT_tokens(parity(o), chunk, o % PAIRS), oT_psum(chunk), ACT.Copy)
                    last.then_inc(act_oT, 1)
                if exists(i - O_LAG):
                    reach(act, dve_norm, i - O_LAG + 1)
                    nc.scalar.activation(o_split[:, :, 0:CH], o_sb[(s - O_LAG) % 2][:, :, :], ACT.Copy)\
                        .then_inc(act_o, 1)
                if exists(i + 1):
                    reach(act, pe_k, i + 2)
                    for j in range(NJ):
                        last = nc.scalar.activation(by_window(k_hi[(s + 1) % 2], j), by_window(ps_k, j),
                                                    ACT.Identity, bias=b_qk[:, 2 + j:3 + j])
                    last.then_inc(act_k, 1)
                if exists(i + SPLIT_LEAD):
                    reach(act, pool_norm, i + SPLIT_LEAD + 1)
                    x_s = s + SPLIT_LEAD
                    nc.scalar.activation(x_step(x_split, x_s)[:, :, 0:CH], x_step(x_norm, x_s), ACT.Copy)\
                        .then_inc(act_x, 1)
                if exists(i):
                    reach(act, pe_scoresT, i + 1)
                    reach(act, pool_p, i)
                    nc.scalar.activation(probs[:, :].rearrange("p (g a n) -> p g a n", g=NG, a=4), scores(),
                                         ACT.Exp, bias=exp_shift[0:TOK, :], scale=exp_scale[0:TOK, :])\
                        .then_inc(act_exp, 1)
                if exists(i + X_LEAD):
                    reach(act, pe_xT, i + X_LEAD + 1)
                    t0, n = STEP_TILES[(s + X_LEAD) % PAIRS]
                    for c in range(n):
                        for chunk in range(3):
                            last = nc.scalar.activation(xT_tokens(parity(s + X_LEAD), chunk, t0 + c),
                                                        xT_psum(chunk, c), ACT.Copy)
                    last.then_inc(act_xT, 1)

            slots(act, slot)

        @block.vector
        def _(dve):
            chained = [0]

            def link(instruction):
                chained[0] += 1
                instruction.then_inc(setup_chain, 1)
                dve.wait_ge(setup_chain, chained[0])

            tt, ts = nc.vector.tensor_tensor, nc.vector.tensor_scalar
            for k in PARTS:
                nc.vector.memset(wqk[k][:, :, :, :], 0.0)
            nc.vector.memset(neg_max[:, :, :, :].bitcast(mybir.dt.uint32), 0)
            nc.vector.memset(exp_shift[:, :], LOG_SHIFT)
            for p in range(V_BUFS):
                nc.vector.memset(v_hi[p][:, :, HD:HD + 1], 1.0)
                nc.vector.memset(v_lo[p][:, :, HD:HD + 1], 0.0)
            for t in (q_hi, q_lo, *k_hi, *k_lo):
                nc.vector.memset(t[:, :], 0.0)
            for t in (*p_lo, *p_hi):
                nc.vector.memset(t[:, NG * 4 * TOK:], 0.0)
            for p in range(2):
                last = nc.vector.memset(xT[p][:, :, COLS:], 0.0)
            link(last)
            dve.wait_ge(dma_w, 9 * 16)
            dve.wait_ge(dma_bqk, 2 * NG * 16)
            link(nc.vector.memset(big_parts[:, :, :], 0.0))

            def magnitude(kind, n, t):
                return nc.vector.tensor_reduce(big_parts[:, kind, n:n + 1], t, AXIS.X, ALU.max,
                                               apply_absolute_value=True)

            for kind in range(3):
                magnitude(kind, 0, wA[:, kind * CH:(kind + 1) * CH])
                last = magnitude(kind, 1, wB[:, kind * CH:(kind + 1) * CH])
            magnitude(3, 0, pA[:, :])
            magnitude(3, 1, pB[:, :])
            for kind in range(2):
                last = magnitude(kind, 2, b_qk[:, 2 * kind:2 * kind + 2])
            link(last)
            link(ts(big_parts[:, 0:2, 2:3], big_parts[:, 0:2, 2:3], 1.0 / 64, None, ALU.mult))
            link(nc.vector.tensor_reduce(big_own[:, :], big_parts[:, :, :], AXIS.X, ALU.max))
            link(ts(big_own[:, :], big_own[:, :], 1e-30, None, ALU.max))
            ts(big_own[:, 0:2], big_own[:, 0:2], MARGIN, None, ALU.mult).then_inc(weights_big, 1)
            dve.wait_ge(weights_big, 2)
            link(nc.vector.reciprocal(big_inv[:, :], big[:, :]))
            link(tt(exp_scale[:, :], big[:, 0:1], big[:, 1:2], ALU.mult))
            link(ts(exp_scale[:, :], exp_scale[:, :], float(HD) ** -0.5, None, ALU.mult))
            link(tt(out_scale[:, :], big[:, 2:3], big[:, 3:4], ALU.mult))
            for kind in range(2):
                b2 = b_qk[:, 2 * kind:2 * kind + 2]
                link(nc.vector.scalar_tensor_tensor(out=b2, in0=b2, scalar=big_inv[:, kind:kind + 1],
                                                    in1=aug[:, 2 * kind:2 * kind + 2], op0=ALU.mult, op1=ALU.add))
            nc.vector.tensor_copy(bvA_rep[:, :], bvA[:, 0:1].broadcast_to([CA, PART]))
            nc.vector.tensor_copy(bvB_rep[:, :], bvB[:, 0:1].broadcast_to([CB, PART])).then_inc(setup_w, 1)
            dve.wait_ge(pe_bias, 1)
            link(nc.vector.tensor_copy(bias_out[:, :], ps_a[0:PART, 0:CH]))
            for kind in range(3):
                for w in (wA, wB):
                    part = w[:, kind * CH:(kind + 1) * CH]
                    link(ts(part, part, big_inv[:, kind:kind + 1], None, ALU.mult))
            for w in (pA, pB):
                link(ts(w[:, :], w[:, :], big_inv[:, 3:4], None, ALU.mult))

            def spread(t):
                return t[:, :, :, :].rearrange("p a g e -> p (a g) e")[:, :, 0:HD]

            def heads(w):
                return w[:, 0:2 * CH].rearrange("p (h d) -> p h d", d=HD)

            for src, hi, lo in ((heads(wA), spread(wqk["hiA"]), spread(wqk["loA"])),
                                (heads(wB), spread(wqk["hiB"]), spread(wqk["loB"])),
                                (wA[:, 2 * CH:], wv["hiA"][:, :], wv["loA"][:, :]),
                                (wB[:, 2 * CH:], wv["hiB"][:, :], wv["loB"][:, :]),
                                (pA[:, :], wp["hiA"][:, :], wp["loA"][:, :]),
                                (pB[:, :], wp["hiB"][:, :], wp["loB"][:, :])):
                link(nc.vector.tensor_copy(hi, src))
                link(tt(lo, src, hi, ALU.subtract))
            dve.wait_ge(pool_const, 7)
            link(nc.vector.tensor_copy(ident16[:, :], ident[:, :]))
            ts(ident_aug[:, :], ident[0:TOK, 0:TOKE], 1.0 / AUG_ONE, None, ALU.mult).then_inc(setup_w, 1)

            n_part = HALF * GCH // 2
            with dve.Fori(0, BATCH) as b:
                for h in range(2):
                    dve.wait_ge(dma_stat[h], b * 16 + 16)
                    for g in range(GROUPS):
                        last = nc.vector.bn_stats(stat6[:, bass.ds(b, 1), h, g, :].rearrange("p b e -> p (b e)"),
                                                  x_stat[h][:, :, GCH * g:GCH * (g + 1)])
                    last.then_inc(stat_read, 1)

            def sum_pairs():
                for n, bank in enumerate((ps_q, ps_k)):
                    v = bank[0:PART, :].rearrange("p (b h g e) -> p b g h e", b=BATCH // 2, h=2, g=GROUPS)
                    size = BATCH // 2 * GROUPS
                    last = nc.vector.tensor_reduce(st_sum[:, n * size:(n + 1) * size]
                                                   .rearrange("p (b g) -> p b g", g=GROUPS), v, AXIS.XY, ALU.add)
                link(last)

            dve.wait_ge(pe_stat, 2)
            sum_pairs()
            link(ts(mean_all[:, :], st_sum[:, :], 1.0 / (4 * PART), None, ALU.mult))
            means = mean_all[:, :].rearrange("p (b g) -> p b g", g=GROUPS).unsqueeze(3)\
                .broadcast_to([PART, BATCH, GROUPS, 2])
            parts = stat6[:, :, :, :, :].rearrange("p b h g (e t) -> p b h g e t", e=2)
            for h in range(2):
                last = tt(st_dev[:, :, h, :, :], parts[:, :, h, :, :, 1], means, ALU.subtract)
            link(last)
            link(tt(st_sq[:, :, :, :, :], st_dev[:, :, :, :, :], st_dev[:, :, :, :, :], ALU.mult))
            for h in range(2):
                last = nc.vector.scalar_tensor_tensor(out=st_dev[:, :, h, :, :], in0=st_sq[:, :, h, :, :],
                                                      scalar=float(n_part), in1=parts[:, :, h, :, :, 2],
                                                      op0=ALU.mult, op1=ALU.add)
            last.then_inc(dve_stat, 1)
            dve.wait_ge(pe_stat, 4)
            sum_pairs()
            ts(var_all[:, :], st_sum[:, :], 1.0 / (4 * PART * n_part), EPS, ALU.mult, ALU.add).then_inc(dve_stat, 1)
            dve.wait_ge(act_sqrt, 1)
            link(nc.vector.reciprocal(rstd_all[:, :], rstd_all[:, :]))
            link(tt(newton[:, :], rstd_all[:, :], rstd_all[:, :], ALU.mult))
            link(tt(newton[:, :], newton[:, :], var_all[:, :], ALU.mult))
            link(ts(newton[:, :], newton[:, :], -0.5, 1.5, ALU.mult, ALU.add))
            tt(rstd_all[:, :], rstd_all[:, :], newton[:, :], ALU.mult).then_inc(stats_done, 1)
            nc.vector.nop().then_inc(setup_done, 1)

            def lo_part(dst, psum, hi, bias=None):
                if bias is None:
                    return tt(dst, psum, hi, ALU.subtract)
                return nc.vector.scalar_tensor_tensor(out=dst, in0=psum, scalar=bias, in1=hi,
                                                      op0=ALU.add, op1=ALU.subtract)

            def slot(base, s):
                i = base + s
                if exists(i):
                    reach(dve, pe_scores, i + 1)
                    nc.vector.tensor_reduce(neg_max[:, :, :, HD:HD + 1].rearrange("p a g e -> p g (a e)"),
                                            scores(), AXIS.X, ALU.max, negate=True).then_inc(dve_max, 1)
                if exists(i):
                    reach(dve, pe_max, i + 1)
                    for j in range(NJ):
                        last = lo_part(by_window(q_lo, j), by_window(ps_q, j), by_window(q_hi, j), b_qk[:, j:j + 1])
                    last.then_inc(dve_q, 1)
                if exists(i + 1):
                    reach(dve, act_k, i + 2)
                    k_now = (s + 1) % 2
                    for j in range(NJ):
                        last = lo_part(by_window(k_lo[k_now], j), by_window(ps_k, j), by_window(k_hi[k_now], j),
                                       b_qk[:, 2 + j:3 + j])
                    last.then_inc(dve_k, 1)
                if exists(i - AV_LAG):
                    reach(dve, pe_av, i - AV_LAG + 1)
                    reach(dve, pool_o, i - AV_LAG - 1)
                    av = ps_a[0:TOK, 0:2 * HEADS * (HD + 1)].rearrange("p (h e) -> p h e", e=HD + 1)
                    nc.vector.reciprocal(recip[:, :, :], av[:, :, HD:HD + 1]).then_inc(dve_recip, 1)
                    reach(dve, dve_recip, i - AV_LAG + 1)
                    tt(o_sb[(s - AV_LAG) % 2][:, :, :].rearrange("p w (h d) -> p (w h) d", d=HD), av[:, :, 0:HD],
                       recip[:, :, :].broadcast_to([TOK, 2 * HEADS, HD]), ALU.mult).then_inc(dve_norm, 1)
                if exists(i - P_LAG):
                    r = s - P_LAG
                    reach(dve, pe_proj, i - P_LAG + 1)
                    reach(dve, pool_y, i - P_LAG + 1)
                    y = x_step(y_blk, r)
                    nc.vector.scalar_tensor_tensor(
                        out=y, in0=ps_b[0:PART, 0:STEP_TILES[r % PAIRS][1] * CH].rearrange("p (c d) -> p c d", d=CH),
                        scalar=out_scale[0:PART, :], in1=y, op0=ALU.mult, op1=ALU.add).then_inc(dve_out, 1)
                if exists(i + 1):
                    reach(dve, pe_q, i + 2)
                    for j in range(NJ):
                        last = ts(by_window(q_hi, j), by_window(ps_q, j), b_qk[:, j:j + 1], None, ALU.add)
                    last.then_inc(dve_q_hi, 1)
                if exists(i + 1):
                    v_now = (s + 1) % V_BUFS
                    v_psum = ps_a[0:TOK, 0:2 * CH].rearrange("p (h d) -> p h d", d=HD)
                    reach(dve, pe_v, i + 2)
                    nc.vector.tensor_copy(v_hi[v_now][:, :, 0:HD], v_psum).then_inc(dve_v_hi, 1)
                    reach(dve, dve_v_hi, i + 2)
                    lo_part(v_lo[v_now][:, :, 0:HD], v_psum, v_hi[v_now][:, :, 0:HD]).then_inc(dve_v, 1)

            slots(dve, slot)

        @block.tensor
        def _(pe):
            mm = nc.tensor.matmul
            pe.wait_ge(setup_w, 1)
            mm(ps_a[0:PART, 0:CH], bvA_rep[:, :], pA[:, :], start=True, stop=False)
            mm(ps_a[0:PART, 0:CH], bvB_rep[:, :], pB[0:CB, :], start=False, stop=False)
            mm(ps_a[0:PART, 0:CH], ones[0:1, :], b_proj[:, :], start=False, stop=True).then_inc(pe_bias, 1)

            mean_v = stat6[:, :, :, :, :].rearrange("p b h g (e t) -> p (b h g) e t", e=2)[:, :, :, 1]
            half = BATCH * GROUPS
            pe.wait_ge(stat_read, 2 * BATCH)
            for n, bank in enumerate((ps_q, ps_k)):
                mm(bank[0:PART, :].rearrange("p (a e) -> p a e", e=2), ones[0:PART, :],
                   mean_v[:, n * half:(n + 1) * half, :], start=True, stop=True).then_inc(pe_stat, 1)
            pe.wait_ge(dve_stat, 1)
            for n, bank in enumerate((ps_q, ps_k)):
                mm(bank[0:PART, :], ones[0:PART, :],
                   st_dev[:, n * BATCH // 2:(n + 1) * BATCH // 2, :, :, :].rearrange("p b h g e -> p (b h g e)"),
                   start=True, stop=True).then_inc(pe_stat, 1)
            pe.wait_ge(setup_w, 2)
            pe.wait_ge(setup_done, 1)

            def products(dst, pairs, first=True, closes=True):
                for n, (lhsT, rhs) in enumerate(pairs):
                    last = mm(dst, lhsT, rhs, start=first and n == 0, stop=closes and n == len(pairs) - 1,
                              skip_group_check=True)
                return last

            def chunks(t, w, rows_are_tokens):
                both = ((t[:, A_HI, :], w["hiA"]), (t[:, A_HI, :], w["loA"]), (t[:, A_LO, :], w["hiA"]),
                        (t[:, B_BOTH, :], w["hiB"]), (t[0:CB, B_BOTH, :], w["loB"][0:CB, :]))
                return both if rows_are_tokens else tuple((b, a) for a, b in both)

            def qk_projection(bank, which, j, s):
                at = 2 * (s % PAIRS) * TOK
                tokens = xT[parity(s)][:, :, at:at + 2 * TOK]
                w = {k: wqk[k][:, 2 * which + j, :, :].rearrange("p g e -> p (g e)") for k in PARTS}
                return products(by_window(bank, j), chunks(tokens, w, False), first=j == 0)

            def attention_output(s, w):
                v_now, p_now = s % V_BUFS, s % 2
                for j in range(NJ):
                    for g in range(NG):
                        h, at = HEADS * w + NG * j + g, (4 * g + 2 * w + j) * TOK
                        last = products(ps_a[:, h * (HD + 1):(h + 1) * (HD + 1)], (
                            (p_hi[p_now][:, at:at + FULL], v_hi[v_now][:, h, :]),
                            (p_hi[p_now][:, at:at + FULL], v_lo[v_now][:, h, :]),
                            (p_lo[p_now][:, at:at + FULL], v_hi[v_now][:, h, :])))
                return last

            def keep_busy(bank, n):
                w = wqk["hiA"]
                for _ in range(n):
                    mm(bank, w[:, 0, :, :].rearrange("p g e -> p (g e)"), w[:, :, :, :].rearrange("p a g e -> p (a g e)"),
                       start=True, stop=True)

            def rows(g):
                return slice(ROW_G * g, ROW_G * g + AUG)

            def transposed_scores(s, w):
                k_now = s % 2
                for j in range(NJ):
                    a, at = (2 * j + w) * TOKE, (2 * w + j) * TOKE
                    for n, (k, q) in enumerate(((k_hi[k_now], q_hi), (k_lo[k_now], q_hi), (k_hi[k_now], q_lo))):
                        for g in range(NG):
                            last = mm(ps_s[:, g, at:at + TOK], k[rows(g), a:a + FULL], q[rows(g), a:a + TOK],
                                      start=n == 0, stop=n == 2)
                return last

            def slot(base, s):
                i = base + s
                if exists(i):
                    reach(pe, dve_q_hi, i + 1)
                    reach(pe, act_k, i + 1)
                    reach(pe, act_exp, i)
                    for w in range(2):
                        for j in range(NJ):
                            a, at = (2 * j + w) * TOKE, (2 * w + j) * TOKE
                            for g in range(NG):
                                last = mm(ps_s[:, g, at:at + TOK], q_hi[rows(g), a:a + FULL],
                                          k_hi[s % 2][rows(g), a:a + TOK], start=True, stop=True)
                    last.then_inc(pe_scores, 1)
                if exists(i + 1):
                    if (s + 1) % PAIRS == 0:
                        reach(pe, act_xT, i + 1 + PAIRS)
                    reach(pe, dve_k, i + 1)
                    keep_busy(ps_k[:, :], 1)
                    qk_projection(ps_k, 1, 0, s + 1)
                if exists(i - AV_LAG):
                    reach(pe, pool_p, i - AV_LAG + 1)
                    if exists(i):
                        reach(pe, dve_v, i + 1)
                    else:
                        reach(pe, dve_norm, i - AV_LAG)
                    attention_output(s - AV_LAG, 0)
                if exists(i - T_LAG):
                    reach(pe, pool_o, i - T_LAG + 1)
                    if exists(i - 1 + X_LEAD):
                        reach(pe, act_xT, i + X_LEAD)
                    else:
                        reach(pe, dve_out, i - P_LAG)
                    for chunk in range(3):
                        for w in range(2):
                            at = (2 * chunk + w) * TOKE
                            last = nc.tensor.transpose(ps_b16[:, at:at + TOK],
                                                       o_split[:, w, chunk * 128:(chunk + 1) * 128],
                                                       ident16[0:TOK, 0:TOK])
                    last.then_inc(pe_oT, 1)
                if exists(i + 1):
                    qk_projection(ps_k, 1, 1, s + 1).then_inc(pe_k, 1)
                if exists(i - AV_LAG):
                    attention_output(s - AV_LAG, 1).then_inc(pe_av, 1)
                if exists(i):
                    reach(pe, dve_max, i + 1)
                    for w in range(2):
                        for j in range(NJ):
                            at = (2 * j + w) * TOKE
                            last = mm(ps_q[:, at:at + TOKE],
                                      neg_max[:, 2 * w + j, :, :].rearrange("p g e -> p (g e)"), ident_aug[:, :],
                                      start=False, stop=True, skip_group_check=True)
                    last.then_inc(pe_max, 1)
                if exists(i - P_LAG):
                    if exists(i - T_LAG):
                        reach(pe, act_oT, i - T_LAG + 1)
                    else:
                        reach(pe, dve_out, i - P_LAG)
                    r = s - P_LAG
                    t0, n = STEP_TILES[r % PAIRS]
                    for c in range(n):
                        weights = {k: wp[k][:, :] for k in PARTS}
                        last = products(ps_b[0:PART, c * CH:(c + 1) * CH],
                                        chunks(oT[parity(r)][:, :, t0 + c, :], weights, True))
                    last.then_inc(pe_proj, 1)
                if exists(i):
                    keep_busy(ps_s[:, 0, :], 3 - STEP_TILES[(s - P_LAG) % PAIRS][1])
                    reach(pe, dve_q, i + 1)
                    transposed_scores(s, 0)
                    transposed_scores(s, 1).then_inc(pe_scoresT, 1)
                if exists(i + 1):
                    reach(pe, dve_q, i + 1)
                    qk_projection(ps_q, 0, 0, s + 1)
                    qk_projection(ps_q, 0, 1, s + 1).then_inc(pe_q, 1)
                if exists(i + 1):
                    if exists(i - AV_LAG):
                        reach(pe, dve_norm, i - AV_LAG + 1)
                    else:
                        reach(pe, dve_v, i + 1)
                    buf, pair = parity(s + 1), (s + 1) % PAIRS
                    for w in range(2):
                        at = (2 * pair + w) * TOK
                        weights = {k: wv[k][:, :] for k in PARTS}
                        last = products(ps_a[:, w * CH:(w + 1) * CH],
                                        chunks(xT[buf][:, :, at:at + FULL], weights, True))
                    last.then_inc(pe_v, 1)
                if exists(i + X_LEAD):
                    reach(pe, dve_out, i - P_LAG + 1)
                    if not exists(i - P_LAG):
                        reach(pe, act_oT, i - T_LAG + 1)
                        reach(pe, act_xT, i + X_LEAD)
                    x_s = s + X_LEAD
                    reach(pe, pool_x, i + X_LEAD + 1)
                    t0, n = STEP_TILES[x_s % PAIRS]
                    for c in range(n):
                        for chunk in range(3):
                            at = (3 * c + chunk) * PART
                            last = nc.tensor.transpose(ps_b16[:, at:at + PART],
                                                       x_split[parity(x_s)][:, t0 + c, chunk * 128:(chunk + 1) * 128],
                                                       ident16[0:PART, 0:PART])
                    last.then_inc(pe_xT, 1)

            slots(pe, slot)


def kernel(x, L0_conv_qkv_w, L0_conv_qkv_b, L0_conv_proj_w, L0_conv_proj_b):
    import numpy as np
    import concourse.bacc as bacc
    from concourse.bass_utils import run_bass_kernel_spmd

    nc = bacc.Bacc("TRN2", target_bir_lowering=False, num_devices=1)
    given = {"x": x, "qkv_w": L0_conv_qkv_w, "qkv_b": L0_conv_qkv_b, "proj_w": L0_conv_proj_w, "proj_b": L0_conv_proj_b}
    arrays = {f"in_{name}": np.ascontiguousarray(a) for name, a in given.items()}
    args = [nc.dram_tensor(name, a.shape, mybir.dt.from_np(a.dtype), kind="ExternalInput").ap()
            for name, a in arrays.items()]
    out = nc.dram_tensor("out", (BATCH, HEIGHT, WIDTH, CH), F32, kind="ExternalOutput").ap()
    window_attention(nc, *args, out)
    result = run_bass_kernel_spmd(nc, [arrays], core_ids=[0])
    return result.results[0]["out"]
```
